# Optimizing a Trainium2 kernel written in Bass

```python
import numpy as np
import jax
import jax.numpy as jnp

def _softmax(x, axis=-1):
    return jax.nn.softmax(x, axis=axis)

def _gelu(x):
    return jax.nn.gelu(x, approximate=True)

def _silu(x):
    return jax.nn.silu(x)

def _sigmoid(x):
    return jax.nn.sigmoid(x)

def _layernorm(x, axis=-1, eps=1e-05):
    m = jnp.mean(x, axis=axis, keepdims=True)
    v = jnp.var(x, axis=axis, keepdims=True)
    return (x - m) / jnp.sqrt(v + eps)

def _scatter_add(tgt, idx, src, axis=0):
    return tgt.at[idx].add(src)

def _segment_sum(src, seg, n):
    return jax.ops.segment_sum(src, seg, n)
kernel_name = 'mk_xattn_ffn_d1_seqx_r8_72e220'

def setup_inputs(seed: int=0):
    np.random.seed(seed)
    _w = jnp.asarray

    def _rec_inputs():
        import jax
        import jax.numpy as jnp
        _rk = jax.random.key(seed)
        x = -0.0003929 + 0.9999 * jax.random.normal(jax.random.fold_in(_rk, 1), (64, 64, 128), jnp.float32)
        _lenS = 64 - jax.random.randint(jax.random.fold_in(_rk, 7), (64,), 0, max(1, 64 // 4) + 1, jnp.int32)
        _lenS2 = 64 - jax.random.randint(jax.random.fold_in(_rk, 8), (64,), 0, max(1, 64 // 4) + 1, jnp.int32)
        _ctx_1024P = jax.random.normal(jax.random.fold_in(_rk, 11), (64, 16, 128), jnp.float32)
        _ctx_1024c = jax.random.dirichlet(jax.random.fold_in(_rk, 511), 0.3 * jnp.ones((16,), jnp.float32), (64, 64))
        _ctx_1024t = jnp.einsum('bsk,bkd->bsd', _ctx_1024c, _ctx_1024P)
        _ctx_1024t = _ctx_1024t * jax.lax.rsqrt(jnp.mean(jnp.square(_ctx_1024t)) + 1e-12) * 0.953939
        ctx_1024 = 2.81802e-05 + 1.00001 * (_ctx_1024t + 0.3 * jax.random.normal(jax.random.fold_in(_rk, 611), (64, 64, 128), jnp.float32))
        _validS = jnp.arange(64)[None, :] < _lenS[:, None]
        _validS2 = jnp.arange(64)[None, :] < _lenS2[:, None]
        _causal = jnp.tril(jnp.ones((64, 64), dtype=bool))
        mask_BxS2_ff1 = jnp.where(jnp.ones((64, 64), dtype=bool), 1.0, 0.0).astype(jnp.float32)
        return (x, ctx_1024, mask_BxS2_ff1)
    x, ctx_1024, mask_BxS2_ff1 = _rec_inputs()

    def _L0_xattn_setup():
        import jax, jax.numpy as jnp
        import numpy as np
        D_MODEL = 128
        HEADS = 16
        DEPTH = D_MODEL // HEADS
        B, S = (4, 512)
        EPS_K = 1e-06
        EPS_LN = 1e-06

        def _layernorm(x, g, b):
            m = jnp.mean(x, axis=-1, keepdims=True)
            var = jnp.var(x, axis=-1, keepdims=True)
            return (x - m) * jax.lax.rsqrt(var + EPS_LN) * g + b

        def _split_heads(x):
            bsz, sl, _ = x.shape
            return x.reshape(bsz, sl, HEADS, DEPTH).transpose(0, 2, 1, 3)
        key = jax.random.key(seed)
        ks = jax.random.split(key, 8)
        lecun = 1.0 / np.sqrt(D_MODEL)
        glorot = np.sqrt(2.0 / (D_MODEL + D_MODEL))
        return {'q': jax.random.normal(ks[0], (B, S, D_MODEL), jnp.float32), 'k': jax.random.normal(ks[1], (B, S, D_MODEL), jnp.float32), 'v': jax.random.normal(ks[2], (B, S, D_MODEL), jnp.float32), 'mask': jnp.ones((B, S), jnp.float32), 'wq': jax.random.normal(ks[3], (D_MODEL, D_MODEL), jnp.float32) * lecun, 'wk': jax.random.normal(ks[4], (D_MODEL, D_MODEL), jnp.float32) * lecun, 'wv': jax.random.normal(ks[5], (D_MODEL, D_MODEL), jnp.float32) * lecun, 'ln_gamma': jnp.ones((D_MODEL,), jnp.float32), 'ln_beta': jnp.zeros((D_MODEL,), jnp.float32), 'dense_w': jax.random.normal(ks[6], (D_MODEL, D_MODEL), jnp.float32) * glorot, 'dense_b': jnp.zeros((D_MODEL,), jnp.float32)}
    _L0_xattn_all = _L0_xattn_setup()
    _L0_xattn_in = {k: v for k, v in _L0_xattn_all.items() if k in ('wq', 'wk', 'wv', 'ln_gamma', 'ln_beta', 'dense_w', 'dense_b')}
    del _L0_xattn_all

    def _L0_ffn_setup():
        import jax, jax.numpy as jnp
        import numpy as np
        N_HEAD = 16
        NUM_EXPERTS = 8
        TOP_K = 2
        LN_EPS = 1e-05

        def _layernorm(x, g, b):
            mu = jnp.mean(x, axis=-1, keepdims=True)
            var = jnp.mean(jnp.square(x - mu), axis=-1, keepdims=True)
            return (x - mu) * jax.lax.rsqrt(var + LN_EPS) * g + b

        def _attention(h, Wq, bq, Wk, bk, Wv, bv, Wp, bp):
            B, T, D = h.shape
            hd = D // N_HEAD

            def split(z):
                return z.reshape(B, T, N_HEAD, hd).transpose(0, 2, 1, 3)
            q = split(h @ Wq + bq)
            k = split(h @ Wk + bk)
            v = split(h @ Wv + bv)
            att = jnp.einsum('bhqd,bhkd->bhqk', q, k) / jnp.sqrt(jnp.float32(hd))
            causal = jnp.tril(jnp.ones((T, T), bool))
            att = jnp.where(causal, att, -jnp.inf)
            att = jax.nn.softmax(att, axis=-1)
            y = jnp.einsum('bhqk,bhkd->bhqd', att, v)
            y = y.transpose(0, 2, 1, 3).reshape(B, T, D)
            return y @ Wp + bp

        def _token_moe(h, gate_W, gate_b, exp_W1, exp_b1, exp_W2, exp_b2):
            B, T, D = h.shape
            flat = h.reshape(-1, D)
            N = flat.shape[0]
            logits = flat @ gate_W + gate_b
            top_v, top_i = jax.lax.top_k(logits, TOP_K)
            w = jax.nn.softmax(top_v, axis=-1)
            w_full = jnp.zeros((N, NUM_EXPERTS), flat.dtype)
            w_full = w_full.at[jnp.arange(N)[:, None], top_i].add(w)
            out = jnp.zeros_like(flat)
            for e in range(NUM_EXPERTS):
                mid = jax.nn.gelu(flat @ exp_W1[e] + exp_b1[e], approximate=False)
                y_e = mid @ exp_W2[e] + exp_b2[e]
                out = out + w_full[:, e:e + 1] * y_e
            return out.reshape(B, T, D)
        key = jax.random.key(seed)
        B, T, D = (8, 128, 128)
        H = 4 * D
        E = NUM_EXPERTS
        ks = jax.random.split(key, 24)
        s = 0.02
        inp = {'x': jax.random.normal(ks[0], (B, T, D), jnp.float32), 'ln1_g': jnp.ones((D,), jnp.float32), 'ln1_b': jnp.zeros((D,), jnp.float32), 'ln2_g': jnp.ones((D,), jnp.float32), 'ln2_b': jnp.zeros((D,), jnp.float32), 'Wq': jax.random.normal(ks[1], (D, D), jnp.float32) * s, 'bq': jnp.zeros((D,), jnp.float32), 'Wk': jax.random.normal(ks[2], (D, D), jnp.float32) * s, 'bk': jnp.zeros((D,), jnp.float32), 'Wv': jax.random.normal(ks[3], (D, D), jnp.float32) * s, 'bv': jnp.zeros((D,), jnp.float32), 'Wp': jax.random.normal(ks[4], (D, D), jnp.float32) * s, 'bp': jnp.zeros((D,), jnp.float32), 'gate_W': jax.random.normal(ks[5], (D, E), jnp.float32) * s, 'gate_b': jnp.zeros((E,), jnp.float32), 'exp_W1': jax.random.normal(ks[6], (E, D, H), jnp.float32) * s, 'exp_b1': jnp.zeros((E, H), jnp.float32), 'exp_W2': jax.random.normal(ks[7], (E, H, D), jnp.float32) * s, 'exp_b2': jnp.zeros((E, D), jnp.float32)}
        return inp
    _L0_ffn_all = _L0_ffn_setup()
    _L0_ffn_in = {k: v for k, v in _L0_ffn_all.items() if k in ('ln1_g', 'ln1_b', 'ln2_g', 'ln2_b', 'Wq', 'bq', 'Wk', 'bk', 'Wv', 'bv', 'Wp', 'bp', 'gate_W', 'gate_b', 'exp_W1', 'exp_b1', 'exp_W2', 'exp_b2')}
    del _L0_ffn_all
    return {'x': x, 'ctx_1024': ctx_1024, 'mask_BxS2_ff1': mask_BxS2_ff1, 'L0_xattn_wq': _L0_xattn_in['wq'], 'L0_xattn_wk': _L0_xattn_in['wk'], 'L0_xattn_wv': _L0_xattn_in['wv'], 'L0_xattn_ln_gamma': _L0_xattn_in['ln_gamma'], 'L0_xattn_ln_beta': _L0_xattn_in['ln_beta'], 'L0_xattn_dense_w': _L0_xattn_in['dense_w'], 'L0_xattn_dense_b': _L0_xattn_in['dense_b'], 'L0_ffn_ln1_g': _L0_ffn_in['ln1_g'], 'L0_ffn_ln1_b': _L0_ffn_in['ln1_b'], 'L0_ffn_ln2_g': _L0_ffn_in['ln2_g'], 'L0_ffn_ln2_b': _L0_ffn_in['ln2_b'], 'L0_ffn_Wq': _L0_ffn_in['Wq'], 'L0_ffn_bq': _L0_ffn_in['bq'], 'L0_ffn_Wk': _L0_ffn_in['Wk'], 'L0_ffn_bk': _L0_ffn_in['bk'], 'L0_ffn_Wv': _L0_ffn_in['Wv'], 'L0_ffn_bv': _L0_ffn_in['bv'], 'L0_ffn_Wp': _L0_ffn_in['Wp'], 'L0_ffn_bp': _L0_ffn_in['bp'], 'L0_ffn_gate_W': _L0_ffn_in['gate_W'], 'L0_ffn_gate_b': _L0_ffn_in['gate_b'], 'L0_ffn_exp_W1': _L0_ffn_in['exp_W1'], 'L0_ffn_exp_b1': _L0_ffn_in['exp_b1'], 'L0_ffn_exp_W2': _L0_ffn_in['exp_W2'], 'L0_ffn_exp_b2': _L0_ffn_in['exp_b2']}

def reference(x, ctx_1024, mask_BxS2_ff1, L0_xattn_wq, L0_xattn_wk, L0_xattn_wv, L0_xattn_ln_gamma, L0_xattn_ln_beta, L0_xattn_dense_w, L0_xattn_dense_b, L0_ffn_ln1_g, L0_ffn_ln1_b, L0_ffn_ln2_g, L0_ffn_ln2_b, L0_ffn_Wq, L0_ffn_bq, L0_ffn_Wk, L0_ffn_bk, L0_ffn_Wv, L0_ffn_bv, L0_ffn_Wp, L0_ffn_bp, L0_ffn_gate_W, L0_ffn_gate_b, L0_ffn_exp_W1, L0_ffn_exp_b1, L0_ffn_exp_W2, L0_ffn_exp_b2):
    import jax
    import jax.numpy as jnp

    def _L0_xattn_ref(q, k, v, mask, wq, wk, wv, ln_gamma, ln_beta, dense_w, dense_b):
        import jax, jax.numpy as jnp
        import numpy as np
        D_MODEL = 128
        HEADS = 16
        DEPTH = D_MODEL // HEADS
        B, S = (4, 512)
        EPS_K = 1e-06
        EPS_LN = 1e-06

        def _layernorm(x, g, b):
            m = jnp.mean(x, axis=-1, keepdims=True)
            var = jnp.var(x, axis=-1, keepdims=True)
            return (x - m) * jax.lax.rsqrt(var + EPS_LN) * g + b

        def _split_heads(x):
            bsz, sl, _ = x.shape
            return x.reshape(bsz, sl, HEADS, DEPTH).transpose(0, 2, 1, 3)
        bsz = q.shape[0]
        em = mask[:, None, :, None]
        qh = _split_heads(_layernorm(q @ wq, ln_gamma, ln_beta))
        kh = _split_heads(_layernorm(k @ wk, ln_gamma, ln_beta))
        vh = _split_heads(_layernorm(v @ wv, ln_gamma, ln_beta))
        q_prime = jax.nn.relu(qh) + EPS_K
        k_prime = (jax.nn.relu(kh) + EPS_K) * em
        vh = vh * em
        kv = jnp.einsum('bhnd,bhne->bhde', k_prime, vh)
        z = 1.0 / (jnp.einsum('bhnd,bhd->bhn', q_prime, k_prime.sum(axis=-2)) + EPS_K)
        att = jnp.einsum('bhnd,bhde,bhn->bhne', q_prime, kv, z)
        att = att.reshape(bsz, -1, D_MODEL)
        out = att @ dense_w + dense_b
        return _layernorm(out, ln_gamma, ln_beta)

    def _L0_ffn_ref(x, ln1_g, ln1_b, ln2_g, ln2_b, Wq, bq, Wk, bk, Wv, bv, Wp, bp, gate_W, gate_b, exp_W1, exp_b1, exp_W2, exp_b2):
        import jax, jax.numpy as jnp
        import numpy as np
        N_HEAD = 16
        NUM_EXPERTS = 8
        TOP_K = 2
        LN_EPS = 1e-05

        def _layernorm(x, g, b):
            mu = jnp.mean(x, axis=-1, keepdims=True)
            var = jnp.mean(jnp.square(x - mu), axis=-1, keepdims=True)
            return (x - mu) * jax.lax.rsqrt(var + LN_EPS) * g + b

        def _attention(h, Wq, bq, Wk, bk, Wv, bv, Wp, bp):
            B, T, D = h.shape
            hd = D // N_HEAD

            def split(z):
                return z.reshape(B, T, N_HEAD, hd).transpose(0, 2, 1, 3)
            q = split(h @ Wq + bq)
            k = split(h @ Wk + bk)
            v = split(h @ Wv + bv)
            att = jnp.einsum('bhqd,bhkd->bhqk', q, k) / jnp.sqrt(jnp.float32(hd))
            causal = jnp.tril(jnp.ones((T, T), bool))
            att = jnp.where(causal, att, -jnp.inf)
            att = jax.nn.softmax(att, axis=-1)
            y = jnp.einsum('bhqk,bhkd->bhqd', att, v)
            y = y.transpose(0, 2, 1, 3).reshape(B, T, D)
            return y @ Wp + bp

        def _token_moe(h, gate_W, gate_b, exp_W1, exp_b1, exp_W2, exp_b2):
            B, T, D = h.shape
            flat = h.reshape(-1, D)
            N = flat.shape[0]
            logits = flat @ gate_W + gate_b
            top_v, top_i = jax.lax.top_k(logits, TOP_K)
            w = jax.nn.softmax(top_v, axis=-1)
            w_full = jnp.zeros((N, NUM_EXPERTS), flat.dtype)
            w_full = w_full.at[jnp.arange(N)[:, None], top_i].add(w)
            out = jnp.zeros_like(flat)
            for e in range(NUM_EXPERTS):
                mid = jax.nn.gelu(flat @ exp_W1[e] + exp_b1[e], approximate=False)
                y_e = mid @ exp_W2[e] + exp_b2[e]
                out = out + w_full[:, e:e + 1] * y_e
            return out.reshape(B, T, D)
        x = x + _attention(_layernorm(x, ln1_g, ln1_b), Wq, bq, Wk, bk, Wv, bv, Wp, bp)
        x = x + _token_moe(_layernorm(x, ln2_g, ln2_b), gate_W, gate_b, exp_W1, exp_b1, exp_W2, exp_b2)
        return x
    x = x + _L0_xattn_ref(_layernorm(x, axis=-1), ctx_1024, ctx_1024, mask_BxS2_ff1, L0_xattn_wq, L0_xattn_wk, L0_xattn_wv, L0_xattn_ln_gamma, L0_xattn_ln_beta, L0_xattn_dense_w, L0_xattn_dense_b)
    x = x + _L0_ffn_ref(_layernorm(x, axis=-1), L0_ffn_ln1_g, L0_ffn_ln1_b, L0_ffn_ln2_g, L0_ffn_ln2_b, L0_ffn_Wq, L0_ffn_bq, L0_ffn_Wk, L0_ffn_bk, L0_ffn_Wv, L0_ffn_bv, L0_ffn_Wp, L0_ffn_bp, L0_ffn_gate_W, L0_ffn_gate_b, L0_ffn_exp_W1, L0_ffn_exp_b1, L0_ffn_exp_W2, L0_ffn_exp_b2)
    return x

_drawn_inputs = setup_inputs


def setup_inputs(seed=0):
    import zlib

    import numpy as np

    out = dict(_drawn_inputs(seed))
    spreads = {'L0_xattn_ln_gamma': (1.0, 0.2),
     'L0_xattn_ln_beta': (0.0, 0.1),
     'L0_xattn_dense_b': (0.0, 0.1),
     'L0_ffn_ln1_g': (1.0, 0.6),
     'L0_ffn_ln1_b': (0.0, 0.8),
     'L0_ffn_ln2_g': (1.0, 0.6),
     'L0_ffn_ln2_b': (0.0, 0.8),
     'L0_ffn_bq': (0.0, 0.8),
     'L0_ffn_bk': (0.0, 0.8),
     'L0_ffn_bv': (0.0, 0.767),
     'L0_ffn_bp': (0.0, 0.1),
     'L0_ffn_gate_b': (0.0, 0.341),
     'L0_ffn_exp_b1': (0.0, 0.8),
     'L0_ffn_exp_b2': (0.0, 0.278)}
    factors = {'L0_ffn_Wq': 8.0,
     'L0_ffn_Wk': 8.0,
     'L0_ffn_Wv': 5.701,
     'L0_ffn_Wp': 4.148,
     'L0_ffn_exp_W1': 3.643,
     'L0_ffn_exp_W2': 3.274}
    for name, (base, spread) in spreads.items():
        noise = np.random.default_rng([zlib.crc32(name.encode()), seed]).standard_normal(out[name].shape)
        drawn = base * np.exp(spread * noise) if base else spread * noise
        out[name] = jnp.asarray(drawn.astype(out[name].dtype))
    for name, factor in factors.items():
        out[name] = (out[name] * factor).astype(out[name].dtype)
    return out
```

```python
from contextlib import ExitStack

import concourse.bass as bass
from concourse import mybir

ALU = mybir.AluOpType
ACT = mybir.ActivationFunctionType
AX = mybir.AxisListType
F32 = mybir.dt.float32
F32R = mybir.dt.float32r
BF16 = mybir.dt.bfloat16
U32 = mybir.dt.uint32

P = 128
LANES = (0, 1)
EPS_X = 1e-5
EPS_K = 1e-6
EPS_A = 1e-6
MASKED = -1e30


def xattn_attention_moe(nc: bass.Bass, a, out):
    B, S, D = a["x"].shape
    HEADS = 16
    HD = D // HEADS
    TILES = B * S // P
    T = 4
    N = T * P
    GROUPS = TILES // T
    E, _, H = a["L0_ffn_exp_W1"].shape
    CH = H // P
    BPT = P // S
    HG = HEADS // 2
    UNITS = 2 * T
    SCALE = float(HD) ** -0.5
    assert D == P and BPT == 2 and HG * S == 512

    x_v = a["x"].rearrange("(g t b) s d -> g (b s) t d", t=T, b=BPT)
    ctx_v = a["ctx_1024"].rearrange("(g t b) s d -> g (b s) t d", t=T, b=BPT)
    w2_v = a["L0_ffn_exp_W2"].rearrange("e (c p) d -> e p c d", p=P)
    b1_v = a["L0_ffn_exp_b1"].rearrange("e (c p o) -> e c p o", p=P, o=1)
    em_v = a["mask_BxS2_ff1"].rearrange("(g t b) s -> g (b s) t", t=T, b=BPT)
    out_v = out.rearrange("(g t b) s d -> g (b s) t d", t=T, b=BPT)

    with ExitStack() as ctx:
        def sb(name, shape, dt=F32):
            return ctx.enter_context(nc.sbuf_tensor(name, shape, dt))

        def lanes(name, shape, dt=F32):
            return [sb(f"{name}{u}", shape, dt) for u in LANES]

        def sems(names):
            return [ctx.enter_context(nc.semaphore(n)) for n in names.split()]

        bank = [[ctx.enter_context(nc.psum_tensor(f"bank{u}{k}", [P, 512], F32)) for k in range(4)] for u in LANES]

        ident = sb("ident", [P, P])
        ident_bf = sb("ident_bf", [P, P], BF16)
        neg_ident = sb("neg_ident", [P, P], F32R)
        causal = sb("causal", [P, S], BF16)
        head16 = sb("head16", [P, HEADS])
        head8 = sb("head8", [P, HG])
        batch2 = sb("batch2", [P, BPT])
        eps_x = sb("eps_x", [P, T])
        minus_half = sb("minus_half", [P, 3 * T])
        ones_row = sb("ones_row", [1, P])
        iota8 = sb("iota8", [P, E])
        w_raw = sb("w_raw", [P, 4, D])
        w_sum = sb("w_sum", [P, 4])
        wx = sb("wx", [P, 4, D])
        db_raw = sb("db_raw", [1, D])
        db_sum = sb("db_sum", [1, 1])
        db_row = sb("db_row", [1, D])
        wf = sb("wf", [P, 4, D])
        gate_w = sb("gate_w", [P, E])
        gamma_b = sb("gamma_b", [P, D])
        beta_b = sb("beta_b", [P, D])
        cols = sb("cols", [P, 6])
        bq_cols = sb("bq_cols", [P, 2])
        bk_cols = sb("bk_cols", [P, 2])
        bv_b = sb("bv_b", [P, D // 2])
        bp_row = sb("bp_row", [1, D])
        gb_row = sb("gb_row", [1, E])

        x_sb = lanes("x_sb", [P, T, D])
        c_sb = lanes("c_sb", [P, T, D])
        em = lanes("em", [P, T])
        em2 = lanes("em2", [P, T])
        emb = lanes("emb", [P, T, BPT])
        stats = lanes("stats", [P, T, 6])
        mv = lanes("mv", [P, T, 2])
        ve = lanes("ve", [P, 3 * T])
        rs = lanes("rs", [P, 3 * T])
        ve2 = lanes("ve2", [P, T])
        rs2 = lanes("rs2", [P, T])
        ss = lanes("ss", [P, 3 * T])
        sq = lanes("sq", [P, 3, N])
        xn = lanes("xn", [P, T, D])
        xpb = lanes("xpb", [P, T, D])
        xnT = lanes("xnT", [P, N])
        cT = lanes("cT", [P, N])
        qp = lanes("qp", [P, N])
        kp = lanes("kp", [P, T, D])
        vp = lanes("vp", [P, T, D])
        kvz = lanes("kvz", [P, T, BPT, HD + 1, 32])
        den = lanes("den", [P, 2, S])
        zed = lanes("zed", [P, T, D])
        x1 = lanes("x1", [P, T, D])
        h1T = lanes("h1T", [P, T, P])
        qbd = lanes("qbd", [P, 2, T, P])
        kb = lanes("kb", [P, 2, T * S])
        km = lanes("km", [P, 2, HG, T * S])
        vbd = lanes("vbd", [P, T * BPT, HG, 2 * (HD + 1)])
        mx = lanes("mx", [P, 2, HG], F32R)
        pr = lanes("pr", [P, 2, 512])
        pT = lanes("pT", [P, 4, P])
        rden = lanes("rden", [P, HEADS])
        w8 = lanes("w8", [P, T, E])
        top = lanes("top", [P, T, 8])
        topi = lanes("topi", [P, T, 8], U32)
        topf = lanes("topf", [P, T, 2])
        dlt = lanes("dlt", [P, T])
        wgt = lanes("wgt", [P, 2, T])
        hot = lanes("hot", [P, 2, T, E])

        h2T = sb("h2T", [P, GROUPS, N])
        acc = sb("acc", [P, GROUPS, T, D])
        gate = sb("gate", [P, GROUPS, T, E])

        w1 = [sb(f"w1_{e}", [P, H]) for e in range(2)]
        w2 = [sb(f"w2_{e}", [P, CH, D]) for e in range(2)]
        b1 = [sb(f"b1_{e}", [P, CH]) for e in range(2)]
        b2 = [sb(f"b2_{e}", [1, D]) for e in range(2)]
        mid = [km[u][:, 0, :, :].rearrange("p h n -> p (h n)").rearrange("p (c n) -> p c n", c=CH) for u in LANES]

        (setup, w_loaded, consts, w_ready, xs_a, xs_b, x_var, x_rstd, xn_ok, xT_ps,
         cT_ps, xT_ok, cT_ok, q_ps, k_ps, v_ps, sq_ok, ss_ok, y_a, qkv_rstd, qn_ok, kn_ok, vn_ok, kg_ok,
         kb_ok, kp_ok, vg_ok, vb_ok, vp_ok, em2_ok, emb_ok, qT_ps, qr_ok, qp_ok, ks_ps, kv_ps, kvz_ok,
         au_ps, den_a, den_b, att_ok, aT_ps, aT_ok, o_ps, o2_ok, oss_ok, y_b, o_rstd, xpb_ok, og_ok, x1_ok,
         z_var, z_rstd, z_ok, h2v_a, h2v_b, w1_a, h_rstd, h_ok, hT_ps, hT_ok, qf_ps, kf_ps, vf_ps, qbd_ok,
         kf_ok, km_ok, vbd_ok, s_ps, mx_ok, sm_ps, p_ok, pT_ps, pT_ok, pv_ps, rden_ok, y_ok, yT_ps, yT_ok,
         f_ps, xa_ok, a_a, a_b, a_var, a_rstd, a_ok, res_ok, aT2_ps, h2T_ok, kept_ok, lg_ps, lg_ok, top_ok, dl_ok,
         e_ok, w1_ok, w2_ok, hot_a, hot_b, winv_ok, wpair_ok, hotw_ok, tf_ok, topi_ok, gate_ok, mid_ps, mid_ok, y2_ps, acc_ok, stored,
        ) = sems(
            "setup "
            "w_loaded consts w_ready xs_a xs_b x_var x_rstd xn_ok xT_ps cT_ps xT_ok cT_ok "
            "q_ps k_ps v_ps sq_ok ss_ok y_a qkv_rstd qn_ok kn_ok vn_ok kg_ok kb_ok kp_ok vg_ok vb_ok vp_ok em2_ok "
            "emb_ok qT_ps qr_ok qp_ok ks_ps kv_ps kvz_ok au_ps den_a den_b att_ok aT_ps aT_ok o_ps o2_ok oss_ok y_b "
            "o_rstd xpb_ok og_ok x1_ok z_var z_rstd z_ok h2v_a h2v_b w1_a h_rstd h_ok hT_ps hT_ok qf_ps kf_ps vf_ps "
            "qbd_ok kf_ok km_ok vbd_ok s_ps mx_ok sm_ps p_ok pT_ps pT_ok pv_ps rden_ok y_ok yT_ps yT_ok f_ps xa_ok a_a "
            "a_b a_var a_rstd a_ok res_ok aT2_ps h2T_ok kept_ok lg_ps lg_ok top_ok dl_ok e_ok w1_ok w2_ok hot_a hot_b winv_ok "
            "wpair_ok hotw_ok tf_ok topi_ok gate_ok mid_ps mid_ok y2_ps acc_ok stored ")
        x_loaded = sems("x_loaded0 x_loaded1")
        c_loaded = sems("c_loaded0 c_loaded1")
        m_loaded = sems("m_loaded0 m_loaded1")
        w1_loaded = sems("w1_loaded0 w1_loaded1")
        w2_loaded = sems("w2_loaded0 w2_loaded1")
        b1_loaded = sems("b1_loaded0 b1_loaded1")
        b2_loaded = sems("b2_loaded0 b2_loaded1")

        def col(v):
            return v.rearrange("(p o) -> p o", o=1)

        def row(v):
            return v.rearrange("(o n) -> o n", o=1)

        def t4(ap):
            return ap.rearrange("p (t d) -> p t d", t=T)

        def over_d(ap):
            return ap.unsqueeze(2).broadcast_to([P, ap.shape[1], D])

        def over_t(ap):
            return ap.unsqueeze(1).broadcast_to([ap.shape[0], T, ap.shape[1]])

        weights = [
            (w_raw[:, 0, :], a["L0_xattn_wq"]), (w_raw[:, 1, :], a["L0_xattn_wk"]),
            (w_raw[:, 2, :], a["L0_xattn_wv"]), (w_raw[:, 3, :], a["L0_xattn_dense_w"]),
            (db_raw[:, :], row(a["L0_xattn_dense_b"])),
            (wf[:, 0, :], a["L0_ffn_Wq"]), (wf[:, 1, :], a["L0_ffn_Wk"]), (wf[:, 2, :], a["L0_ffn_Wv"]),
            (wf[:, 3, :], a["L0_ffn_Wp"]), (gate_w[:, :], a["L0_ffn_gate_W"]),
            (gamma_b[:, :], row(a["L0_xattn_ln_gamma"]).broadcast_to([P, D])),
            (beta_b[:, :], row(a["L0_xattn_ln_beta"]).broadcast_to([P, D])),
            (cols[:, 0:1], col(a["L0_xattn_ln_gamma"])), (cols[:, 1:2], col(a["L0_xattn_ln_beta"])),
            (cols[:, 2:3], col(a["L0_ffn_ln1_g"])), (cols[:, 3:4], col(a["L0_ffn_ln1_b"])),
            (cols[:, 4:5], col(a["L0_ffn_ln2_g"])), (cols[:, 5:6], col(a["L0_ffn_ln2_b"])),
            (bp_row[:, :], row(a["L0_ffn_bp"])), (gb_row[:, :], row(a["L0_ffn_gate_b"])),
        ]
        for b in range(BPT):
            rows = slice(b * S, b * S + S)
            weights += [
                *((dst[rows, g:g + 1], col(src[g * 64:g * 64 + 64])) for g in range(2)
                  for dst, src in ((bq_cols, a["L0_ffn_bq"]), (bk_cols, a["L0_ffn_bk"]))),
                (bv_b[rows, :].rearrange("p (h d) -> p h d", h=HG),
                 a["L0_ffn_bv"].rearrange("(h b d) -> b h d", b=2, d=HD)[b:b + 1].broadcast_to([S, HG, HD])),
            ]

        with nc.Block() as block:
            @block.sync
            def _(sp):
                for dst, src in weights:
                    sp.dma_start(dst, src).then_inc(w_loaded, 16)

                def load(u, group):
                    sp.dma_start(c_sb[u][:, :, :], ctx_v[group]).then_inc(c_loaded[u], 16)
                    sp.dma_start(x_sb[u][:, :, :], x_v[group]).then_inc(x_loaded[u], 16)
                    sp.dma_start(em[u][:, :], em_v[group], allow_slow_non_contiguous=True).then_inc(m_loaded[u], 16)

                for u in LANES:
                    load(u, u)
                def load_expert(e, expert):
                    sp.dma_start(w1[e][:, :], a["L0_ffn_exp_W1"][expert]).then_inc(w1_loaded[e], 16)
                    sp.dma_start(w2[e][:, :, :], w2_v[expert]).then_inc(w2_loaded[e], 16)
                    sp.dma_start(b2[e][:, :], a["L0_ffn_exp_b2"].rearrange("e (o d) -> e o d", o=1)[expert])\
                      .then_inc(b2_loaded[e], 16)
                    for c in range(CH):
                        sp.dma_start(b1[e][:, c:c + 1], b1_v[expert][c]).then_inc(b1_loaded[e], 16)

                for e in range(2):
                    load_expert(e, e)
                with sp.Fori(0, GROUPS // 2 - 1) as r:
                    g = 2 * r
                    for u in LANES:
                        sp.wait_ge(cT_ps, g + u + 1)
                        sp.wait_ge(em2_ok, g + u + 1)
                        sp.wait_ge(emb_ok, g + u + 1)
                        sp.wait_ge(res_ok, g + u + 1)
                        sp.wait_ge(a_ok, g + u + 1)
                        load(u, g + u + 2)

                with sp.Fori(0, E // 2 - 1) as rep:
                    for e in range(2):
                        sp.wait_ge(y2_ps, (rep * 2 + e + 1) * GROUPS)
                        load_expert(e, rep * 2 + e + 2)
                for g in range(GROUPS):
                    sp.wait_ge(acc_ok, (E - 1) * GROUPS + g + 3)
                    sp.dma_start(out_v[g], acc[:, g, :, :]).then_inc(stored, 16)
                sp.wait_ge(stored, 16 * GROUPS)

            @block.tensor
            def _(pe):
                def per_tile(psum, lhsT_of, rhs, start=True):
                    for t in range(T):
                        last = pe.matmul(t4(psum[:, :])[:, t, :], lhsT_of(t), rhs, start=start, stop=True)
                    return last

                def transposes(psum, src_of):
                    for t in range(T):
                        last = pe.transpose(t4(psum[:, :])[:, t, :], src_of(t), ident[:, :])
                    return last

                def scores(u, n):
                    g, t = n % 2, n // 2
                    s = bank[u][n % 2]
                    pe.matmul(s[:, :], ident_bf[:, :],
                              causal[:, :].unsqueeze(1).broadcast_to([P, HG, S]), start=True, stop=False)
                    k_all = km[u][:, g, :, :].rearrange("p h (t k) -> p h t k", t=T)
                    pe.matmul(s[:, :], qbd[u][:, g, t, :], k_all[:, :, t, :], start=False, stop=True).then_inc(s_ps, 1)

                pe.wait_ge(consts, 1)
                pe.wait_ge(w_ready, 1)
                with pe.Fori(0, GROUPS // 2) as r:
                    g = 2 * r
                    lap = [g + 1 + u for u in LANES]
                    for u in LANES:
                        pe.wait_ge(c_loaded[u], (r + 1) * 16)
                        transposes(bank[u][1], lambda t: c_sb[u][:, t, :]).then_inc(cT_ps, 1)
                        pe.wait_ge(xn_ok, lap[u])
                        transposes(bank[u][0], lambda t: xn[u][:, t, :]).then_inc(xT_ps, 1)
                    for u in LANES:
                        pe.wait_ge(xT_ok, lap[u])
                        per_tile(bank[u][2], lambda t: xnT[u][:, t * P:t * P + P], wx[:, 0, :]).then_inc(q_ps, 1)
                        pe.wait_ge(cT_ok, lap[u])
                        per_tile(bank[u][3], lambda t: cT[u][:, t * P:t * P + P], wx[:, 1, :]).then_inc(k_ps, 1)
                        per_tile(bank[u][0], lambda t: cT[u][:, t * P:t * P + P], wx[:, 2, :]).then_inc(v_ps, 1)
                    for u in LANES:
                        pe.wait_ge(qn_ok, lap[u])
                        transposes(bank[u][1], lambda t: xn[u][:, t, :]).then_inc(qT_ps, 1)
                    for u in LANES:
                        pe.wait_ge(kp_ok, lap[u])
                        pe.wait_ge(emb_ok, lap[u])
                        pe.wait_ge(vn_ok, lap[u])
                        for t in range(T):
                            last = pe.matmul(bank[u][0][:, t * BPT:t * BPT + BPT], kp[u][:, t, :], emb[u][:, t, :],
                                             start=True, stop=True)
                        last.then_inc(ks_ps, 1)
                        pe.wait_ge(vp_ok, lap[u])
                        for b in range(BPT):
                            rows = slice(b * S, b * S + S)
                            for t in range(T):
                                last = pe.matmul(t4(bank[u][2 + b][:, :])[:, t, :], kp[u][rows, t, :],
                                                 vp[u][rows, t, :], start=True, stop=True)
                        last.then_inc(kv_ps, 1)
                    for u in LANES:
                        pe.wait_ge(kvz_ok, lap[u])
                        pe.wait_ge(qp_ok, lap[u])
                        for half in range(2):
                            for c in range(HD + 1):
                                dst = bank[u][1 - half] if c < HD else bank[u][2]
                                at = c * S if c < HD else half * S
                                for b4 in range(4):
                                    t, b = 2 * half + b4 // 2, b4 % 2
                                    last = pe.matmul(dst[b4 * 32:b4 * 32 + 32, at:at + S], kvz[u][:, t, b, c, :],
                                                     qp[u][:, t * P + b * S:t * P + b * S + S],
                                                     start=True, stop=True)
                        last.then_inc(au_ps, 1)
                    for u in LANES:
                        pe.wait_ge(att_ok, lap[u])
                        for half in range(2):
                            for n4 in range(4):
                                last = pe.transpose(bank[u][3 - 2 * half][:, n4 * P:n4 * P + P],
                                                    sq[u][:, half, n4 * P:n4 * P + P], ident[:, :])
                        last.then_inc(aT_ps, 1)
                    for u in LANES:
                        pe.wait_ge(aT_ok, lap[u])
                        pe.matmul(t4(bank[u][3][:, :]), ones_row[:, :], over_t(db_row[:, :]), start=True, stop=True)
                        for t in range(T):
                            last = pe.matmul(t4(bank[u][3][:, :])[:, t, :], xnT[u][:, t * P:t * P + P], wx[:, 3, :],
                                             start=False, stop=True, skip_group_check=True)
                        last.then_inc(o_ps, 1)
                    for u in LANES:
                        pe.wait_ge(h_ok, lap[u])
                        transposes(bank[u][0], lambda t: xn[u][:, t, :]).then_inc(hT_ps, 1)
                    for u in LANES:
                        pe.wait_ge(hT_ok, lap[u])
                        for w, ready in ((0, qf_ps), (1, kf_ps)):
                            for gg in range(2):
                                for b in range(BPT):
                                    last = pe.matmul(
                                        bank[u][1 + w][b * S:b * S + S, gg * T * S:(gg + 1) * T * S]
                                        .rearrange("p (t s) -> p t s", t=T),
                                        wf[:, w, gg * 64:gg * 64 + 64],
                                        h1T[u][:, :, b * S:b * S + S], start=True, stop=True)
                            last.then_inc(ready, 1)
                        wv = wf[:, 2, :].rearrange("p (h b d) -> p b h d", b=2, d=HD)
                        for t in range(T):
                            for b in range(BPT):
                                for odd in range(2):
                                    at = (t * BPT + b) * 64
                                    last = pe.matmul(
                                        bank[u][3][odd * S:odd * S + S, at:at + 64]
                                        .rearrange("p (h d) -> p h d", h=HG),
                                        h1T[u][:, t, b * S:b * S + S], wv[:, odd], start=True, stop=True)
                        last.then_inc(vf_ps, 1)
                    for u in LANES:
                        pe.wait_ge(qbd_ok, lap[u])
                        pe.wait_ge(km_ok, lap[u])
                        pe.wait_ge(vbd_ok, lap[u])
                        scores(u, 0)
                    for n in range(UNITS):
                        gg, t = n % 2, n // 2
                        for u in LANES:
                            pe.wait_ge(mx_ok, (g * UNITS) + 2 * n + u + 1)
                            pe.matmul(bank[u][n % 2][:, :], neg_ident[:, :],
                                      mx[u][:, n % 2, :].unsqueeze(2).broadcast_to([P, HG, S]),
                                      start=False, stop=True, skip_group_check=True).then_inc(sm_ps, 1)
                            if n + 1 < UNITS:
                                if n >= 1:
                                    pe.wait_ge(p_ok, (g * UNITS) + 2 * (n - 1) + u + 1)
                                scores(u, n + 1)
                        for u in LANES:
                            pe.wait_ge(p_ok, (g * UNITS) + 2 * n + u + 1)
                            for j in range(4):
                                last = pe.transpose(bank[u][2][:, j * P:j * P + P], pr[u][:, n % 2, j * P:j * P + P],
                                                    ident[:, :])
                            last.then_inc(pT_ps, 1)
                        for u in LANES:
                            pe.wait_ge(pT_ok, (g * UNITS) + 2 * n + u + 1)
                            if gg == 0 and t >= 1:
                                pe.wait_ge(y_ok, (g * T) + 2 * (t - 1) + u + 1)
                            W = 2 * BPT * (HD + 1)
                            for j in range(4):
                                hp = gg * 4 + j
                                last = pe.matmul(
                                    bank[u][3][:, hp * W:hp * W + W].rearrange("p (b c) -> p b c", b=BPT),
                                    pT[u][:, j, :], vbd[u][:, t * BPT:t * BPT + BPT, hp, :], start=True, stop=True)
                            last.then_inc(pv_ps, 1)
                    for u in LANES:
                        pe.wait_ge(y_ok, (g * T) + 2 * (T - 1) + u + 1)
                        transposes(bank[u][0], lambda t: xn[u][:, t, :]).then_inc(yT_ps, 1)
                    for u in LANES:
                        pe.wait_ge(yT_ok, lap[u])
                        pe.matmul(t4(bank[u][1][:, :]), ones_row[:, :], over_t(bp_row[:, :]), start=True, stop=True)
                        for t in range(T):
                            last = pe.matmul(t4(bank[u][1][:, :])[:, t, :], xnT[u][:, t * P:t * P + P], wf[:, 3, :],
                                             start=False, stop=True, skip_group_check=True)
                        last.then_inc(f_ps, 1)
                    for u in LANES:
                        pe.wait_ge(a_ok, lap[u])
                        transposes(bank[u][2], lambda t: xn[u][:, t, :]).then_inc(aT2_ps, 1)
                    for u in LANES:
                        pe.wait_ge(h2T_ok, lap[u])
                        lg = bank[u][3][:, 0:T * E].rearrange("p (t e) -> p t e", t=T)
                        pe.matmul(lg, ones_row[:, :], over_t(gb_row[:, :]), start=True, stop=True)
                        for t in range(T):
                            last = pe.matmul(lg[:, t, :], h1T[u][:, t, :], gate_w[:, :], start=False, stop=True,
                                             skip_group_check=True)
                        last.then_inc(lg_ps, 1)

                pe.wait_ge(gate_ok, GROUPS)
                pe.wait_ge(kept_ok, GROUPS)
                with pe.Fori(0, E // 2) as rep:
                    for e in range(2):
                        with pe.Fori(0, GROUPS // 2) as r:
                            pe.wait_ge(w1_loaded[e], (rep + 1) * 16)
                            pe.wait_ge(w2_loaded[e], (rep + 1) * 16)
                            pe.wait_ge(b2_loaded[e], (rep + 1) * 16)
                            for u in LANES:
                                item = (rep * 2 + e) * GROUPS + r * 2 + u
                                for c in range(CH + 1):
                                    if c < CH:
                                        if c >= 2:
                                            pe.wait_ge(mid_ok, item * CH + (c - 1))
                                        pe.matmul(bank[u][c % 2][:, :], w1[e][:, c * P:c * P + P],
                                                  h2T[:, r * 2 + u, :], start=True, stop=True).then_inc(mid_ps, 1)
                                    if c == 0:
                                        pe.wait_ge(acc_ok, item + 1)
                                        pe.matmul(t4(bank[u][2][:, :]), ones_row[:, :], over_t(b2[e][:, :]),
                                                  start=True, stop=True)
                                    if c >= 1:
                                        pe.wait_ge(mid_ok, item * CH + c)
                                        for t in range(T):
                                            last = pe.matmul(t4(bank[u][2][:, :])[:, t, :],
                                                             mid[u][:, c - 1, t * P:t * P + P], w2[e][:, c - 1, :],
                                                             start=False, stop=True, skip_group_check=True)
                                last.then_inc(y2_ps, 1)

            @block.scalar
            def _(act):
                A = nc.scalar.activation
                act.wait_ge(consts, 1)
                act.wait_ge(w_ready, 1)
                with act.Fori(0, GROUPS // 2) as r:
                    g = 2 * r
                    lap = [g + 1 + u for u in LANES]
                    for u in LANES:
                        act.wait_ge(cT_ps, lap[u])
                        nc.scalar.copy(cT[u][:, :], bank[u][1][:, :]).then_inc(cT_ok, 1)
                        act.wait_ge(xT_ps, lap[u])
                        nc.scalar.copy(xnT[u][:, :], bank[u][0][:, :]).then_inc(xT_ok, 1)
                    for u in LANES:
                        for w, k, ready in ((0, 2, q_ps), (1, 3, k_ps), (2, 0, v_ps)):
                            act.wait_ge(ready, lap[u])
                            last = A(sq[u][:, w, :], bank[u][k][:, :], ACT.Square)
                        last.then_inc(sq_ok, 1)
                    for u in LANES:
                        act.wait_ge(qT_ps, lap[u])
                        A(qp[u][:, :], bank[u][1][:, :], ACT.Relu, bias=cols[:, 1:2], scale=cols[:, 0:1]).then_inc(qr_ok, 1)
                    for u in LANES:
                        act.wait_ge(aT_ps, lap[u])
                        for half in range(2):
                            last = nc.scalar.copy(
                                xnT[u][:, half * 256:half * 256 + 256].rearrange("p (b h n) -> p n b h", b=4, n=4),
                                bank[u][3 - 2 * half][:, :].rearrange("p (n b x h) -> p n b x h", n=4, b=4, x=2)
                                [:, :, :, 0, :])
                        last.then_inc(aT_ok, 1)
                    for u in LANES:
                        act.wait_ge(o_ps, lap[u])
                        A(sq[u][:, 0, :], bank[u][3][:, :], ACT.Square).then_inc(o2_ok, 1)
                    for u in LANES:
                        act.wait_ge(hT_ps, lap[u])
                        A(h1T[u][:, :, :], t4(bank[u][0][:, :]), ACT.Identity, bias=cols[:, 3:4],
                          scale=cols[:, 2:3]).then_inc(hT_ok, 1)
                    for u in LANES:
                        act.wait_ge(kf_ps, lap[u])
                        for gg in range(2):
                            last = A(kb[u][:, gg, :], bank[u][2][:, gg * T * S:(gg + 1) * T * S], ACT.Identity,
                                     bias=bk_cols[:, gg:gg + 1])
                        last.then_inc(kf_ok, 1)
                    for n in range(UNITS):
                        for u in LANES:
                            act.wait_ge(sm_ps, (g * UNITS) + 2 * n + u + 1)
                            A(pr[u][:, n % 2, :], bank[u][n % 2][:, :], ACT.Exp).then_inc(p_ok, 1)
                        for u in LANES:
                            act.wait_ge(pT_ps, (g * UNITS) + 2 * n + u + 1)
                            if n >= 1:
                                act.wait_ge(pv_ps, (g * UNITS) + 2 * (n - 1) + u + 1)
                            nc.scalar.copy(pT[u][:, :, :], bank[u][2][:, :].rearrange("p (j q) -> p j q", j=4)).then_inc(pT_ok, 1)
                    for u in LANES:
                        act.wait_ge(yT_ps, lap[u])
                        nc.scalar.copy(xnT[u][:, :], bank[u][0][:, :]).then_inc(yT_ok, 1)
                    for u in LANES:
                        act.wait_ge(aT2_ps, lap[u])
                        A(h1T[u][:, :, :], t4(bank[u][2][:, :]), ACT.Identity, bias=cols[:, 5:6],
                          scale=cols[:, 4:5]).then_inc(h2T_ok, 1)
                    for u in LANES:
                        act.wait_ge(dl_ok, lap[u])
                        A(dlt[u][:, :], dlt[u][:, :], ACT.Exp).then_inc(e_ok, 1)

                with act.Fori(0, E // 2) as rep:
                    for e in range(2):
                        act.wait_ge(b1_loaded[e], (rep + 1) * 16 * CH)
                        with act.Fori(0, GROUPS // 2) as r:
                            for u in LANES:
                                item = (rep * 2 + e) * GROUPS + r * 2 + u
                                for c in range(CH):
                                    act.wait_ge(mid_ps, item * CH + (c + 1))
                                    A(mid[u][:, c, :], bank[u][c % 2][:, :], ACT.Gelu,
                                      bias=b1[e][:, c:c + 1]).then_inc(mid_ok, 1)

            @block.gpsimd
            def _(pool):
                G = nc.gpsimd
                steps = [0]

                def step(ins):
                    steps[0] += 1
                    ins.then_inc(setup, 1)
                    pool.wait_ge(setup, steps[0])

                def keep(ap, fill, compare, base, pattern, channel):
                    step(G.affine_select(out=ap, in_=ap, compare_op=compare, fill=fill, base=base,
                                         pattern=pattern, channel_multiplier=channel))

                step(G.memset(minus_half[:, :], -0.5))
                step(G.memset(eps_x[:, :], EPS_X))
                step(G.memset(ones_row[:, :], 1.0))
                step(G.iota(iota8[:, :], pattern=[[1, E]], base=0, channel_multiplier=0,
                            allow_small_or_imprecise_dtypes=True))
                for u in LANES:
                    step(G.memset(qbd[u][:, :, :, :], 0.0))
                    step(G.memset(vbd[u][:, :, :, :], 0.0))
                    step(G.memset(kvz[u][:, :, :, :, :], 0.0))
                for c in (ident, ident_bf):
                    step(G.memset(c[:, :], 0.0))
                    keep(c[:, :], 1.0, ALU.not_equal, 0, [[-1, P]], 1)
                step(G.memset(causal[:, :], 0.0))
                step(G.memset(batch2[:, :], 0.0))
                step(G.memset(head16[:, :], 1.0))
                step(G.memset(head8[:, :], 1.0))
                keep(head16[:, :], 0.0, ALU.is_ge, 0, [[-HD, HEADS]], 1)
                keep(head16[:, :], 0.0, ALU.is_ge, HD - 1, [[HD, HEADS]], -1)
                for b in range(BPT):
                    rows = slice(b * S, b * S + S)
                    keep(causal[rows, :], MASKED, ALU.is_ge, 0, [[-1, S]], 1)
                    keep(head8[rows, :], 0.0, ALU.is_ge, 0, [[-HD, HG]], 1)
                    keep(head8[rows, :], 0.0, ALU.is_ge, HD - 1, [[HD, HG]], -1)
                    step(G.memset(batch2[rows, b:b + 1], 1.0))
                    for u in LANES:
                        at = b * (HD + 1) + HD
                        step(G.memset(vbd[u][rows, :, :, at:at + 1], 1.0))
                G.memset(xpb[0][:, 0, 0:1], 0.0).then_inc(consts, 1)
                pool.wait_ge(w_loaded, 16 * len(weights))

                def inv_sqrt(dst, src, n):
                    return G.tensor_tensor(dst, src, minus_half[:, 0:n], ALU.pow)

                with pool.Fori(0, GROUPS // 2) as r:
                    g = 2 * r
                    lap = [g + 1 + u for u in LANES]
                    for u in LANES:
                        pool.wait_ge(x_var, lap[u])
                        inv_sqrt(rs2[u][:, :], ve2[u][:, :], T).then_inc(x_rstd, 1)
                        pool.wait_ge(m_loaded[u], (r + 1) * 16)
                        G.tensor_tensor(em2[u][:, :], em[u][:, :], em[u][:, :], ALU.mult).then_inc(em2_ok, 1)
                        G.tensor_tensor(xpb[u][:, :, :], x_sb[u][:, :, :], over_t(beta_b[:, :]), ALU.add).then_inc(xpb_ok, 1)
                    for u in LANES:
                        pool.wait_ge(ss_ok, lap[u])
                        inv_sqrt(rs[u][:, :], ve[u][:, :], 3 * T).then_inc(qkv_rstd, 1)
                    for u in LANES:
                        pool.wait_ge(vn_ok, lap[u])
                        pool.wait_ge(em2_ok, lap[u])
                        G.tensor_tensor(vp[u][:, :, :], vp[u][:, :, :], over_t(gamma_b[:, :]), ALU.mult).then_inc(vg_ok, 1)
                        pool.wait_ge(vg_ok, lap[u])
                        G.tensor_tensor(vp[u][:, :, :], vp[u][:, :, :], over_t(beta_b[:, :]), ALU.add).then_inc(vb_ok, 1)
                        pool.wait_ge(vb_ok, lap[u])
                        G.tensor_tensor(vp[u][:, :, :], vp[u][:, :, :], over_d(em2[u][:, :]), ALU.mult).then_inc(vp_ok, 1)
                    for u in LANES:
                        pool.wait_ge(oss_ok, lap[u])
                        inv_sqrt(rs2[u][:, :], ve2[u][:, :], T).then_inc(o_rstd, 1)
                    for u in LANES:
                        pool.wait_ge(z_var, lap[u])
                        inv_sqrt(rs2[u][:, :], ve2[u][:, :], T).then_inc(z_rstd, 1)
                    for u in LANES:
                        pool.wait_ge(z_rstd, lap[u])
                        G.tensor_tensor(ve[u][:, 0:T], rs2[u][:, :], rs2[u][:, :], ALU.mult).then_inc(h2v_a, 1)
                        pool.wait_ge(h2v_a, lap[u])
                        G.tensor_tensor(ve[u][:, T:2 * T], ve[u][:, 0:T], mv[u][:, :, 1], ALU.mult).then_inc(h2v_b, 1)
                        pool.wait_ge(h2v_b, lap[u])
                        G.tensor_tensor(ve[u][:, 2 * T:3 * T], ve[u][:, T:2 * T], eps_x[:, :], ALU.add).then_inc(w1_a, 1)
                        pool.wait_ge(w1_a, lap[u])
                        inv_sqrt(rs[u][:, 0:T], ve[u][:, 2 * T:3 * T], T).then_inc(h_rstd, 1)
                    for u in LANES:
                        pool.wait_ge(xa_ok, lap[u])
                        G.tensor_tensor(acc[:, g + u, :, :], x1[u][:, :, :], x_sb[u][:, :, :], ALU.add).then_inc(res_ok, 1)
                        pool.wait_ge(a_var, lap[u])
                        inv_sqrt(rs2[u][:, :], ve2[u][:, :], T).then_inc(a_rstd, 1)
                    for u in LANES:
                        pool.wait_ge(h2T_ok, lap[u])
                        G.tensor_copy(h2T[:, g + u, :], h1T[u][:, :, :].rearrange("p t n -> p (t n)")).then_inc(kept_ok, 1)

            @block.vector
            def _(dve):
                V = nc.vector

                def moments(src, u, b_sem, var_sem, eps, n):
                    for t in range(T):
                        V.bn_stats(stats[u][:, t, :], src[:, t, :])
                    dve.drain()
                    for t in range(T):
                        last = V.bn_aggr(mv[u][:, t, :], stats[u][:, t, :])
                    last.then_inc(b_sem, 1)
                    dve.wait_ge(b_sem, n)
                    V.tensor_scalar(ve2[u][:, :], mv[u][:, :, 1], eps, None, ALU.add).then_inc(var_sem, 1)

                def normalize(dst, src, u):
                    for t in range(T):
                        last = V.tensor_scalar(dst[:, t, :], src[:, t, :], mv[u][:, t, 0:1], rs2[u][:, t:t + 1],
                                               ALU.subtract, ALU.mult)
                    return last

                dve.wait_ge(w_loaded, 16 * len(weights))
                dve.wait_ge(consts, 1)
                V.tensor_reduce(w_sum[:, :], w_raw[:, :, :], AX.X, ALU.add)
                V.tensor_reduce(db_sum[:, :], db_raw[:, :], AX.X, ALU.add)
                V.tensor_scalar(neg_ident[:, :], ident[:, :], -1.0, None, ALU.mult).then_inc(w1_ok, 1)
                dve.wait_ge(w1_ok, 1)
                V.tensor_scalar(w_sum[:, :], w_sum[:, :], -1.0 / D, None, ALU.mult)
                V.tensor_scalar(db_sum[:, :], db_sum[:, :], -1.0 / D, None, ALU.mult).then_inc(w1_ok, 1)
                dve.wait_ge(w1_ok, 2)
                V.tensor_tensor(wx[:, :, :], w_raw[:, :, :], w_sum[:, :].unsqueeze(2).broadcast_to([P, 4, D]), ALU.add)
                V.tensor_scalar(db_row[:, :], db_raw[:, :], db_sum[:, :], None, ALU.add).then_inc(w_ready, 1)

                with dve.Fori(0, GROUPS // 2) as r:
                    g = 2 * r
                    lap = [g + 1 + u for u in LANES]
                    for u in LANES:
                        dve.wait_ge(x_loaded[u], (r + 1) * 16)
                        moments(x_sb[u], u, xs_b, x_var, EPS_X, lap[u])
                    for u in LANES:
                        dve.wait_ge(x_rstd, lap[u])
                        normalize(xn[u], x_sb[u], u).then_inc(xn_ok, 1)
                        dve.wait_ge(m_loaded[u], (r + 1) * 16)
                        V.tensor_tensor(emb[u][:, :, :], em[u][:, :].unsqueeze(2).broadcast_to([P, T, BPT]),
                                        batch2[:, :].unsqueeze(1).broadcast_to([P, T, BPT]), ALU.mult).then_inc(emb_ok, 1)
                    for u in LANES:
                        dve.wait_ge(sq_ok, lap[u])
                        V.tensor_reduce(ss[u][:, :], sq[u][:, :, :].rearrange("p w (t d) -> p (w t) d", t=T), AX.X,
                                        ALU.add).then_inc(y_a, 1)
                    for u in LANES:
                        dve.wait_ge(y_a, lap[u])
                        V.tensor_scalar(ve[u][:, :], ss[u][:, :], 1.0 / D, EPS_A, ALU.mult, ALU.add).then_inc(ss_ok, 1)
                    for u in LANES:
                        dve.wait_ge(qkv_rstd, lap[u])
                        for w, k, dst, ok in ((0, 2, xn, qn_ok), (2, 0, vp, vn_ok), (1, 3, kp, kn_ok)):
                            V.tensor_tensor(dst[u][:, :, :], t4(bank[u][k][:, :]), over_d(rs[u][:, w * T:w * T + T]),
                                            ALU.mult).then_inc(ok, 1)
                    for u in LANES:
                        dve.wait_ge(kn_ok, lap[u])
                        V.tensor_tensor(kp[u][:, :, :], kp[u][:, :, :], over_t(gamma_b[:, :]), ALU.mult).then_inc(kg_ok, 1)
                    for u in LANES:
                        dve.wait_ge(kg_ok, lap[u])
                        V.tensor_tensor(kp[u][:, :, :], kp[u][:, :, :], over_t(beta_b[:, :]), ALU.add).then_inc(kb_ok, 1)
                    for u in LANES:
                        dve.wait_ge(kb_ok, lap[u])
                        V.tensor_scalar(kp[u][:, :, :], kp[u][:, :, :], 0.0, EPS_K, ALU.max, ALU.add).then_inc(kp_ok, 1)
                        dve.wait_ge(qr_ok, lap[u])
                        V.tensor_scalar(qp[u][:, :], qp[u][:, :], EPS_K, None, ALU.add).then_inc(qp_ok, 1)
                    for u in LANES:
                        dve.wait_ge(ks_ps, lap[u])
                        V.tensor_tensor(
                            kvz[u][:, :, :, HD, 0:HEADS].rearrange("p t b h -> p (t b) h"),
                            bank[u][0][:, 0:T * BPT].unsqueeze(2).broadcast_to([P, T * BPT, HEADS]),
                            head16[:, :].unsqueeze(1).broadcast_to([P, T * BPT, HEADS]), ALU.mult)
                        dve.wait_ge(kv_ps, lap[u])
                        for b in range(BPT):
                            last = V.tensor_tensor(
                                kvz[u][:, :, b, 0:HD, 0:HEADS].rearrange("p t d h -> p t h d"),
                                bank[u][2 + b][:, :].rearrange("p (t h d) -> p t h d", t=T, h=HEADS),
                                head16[:, :].unsqueeze(1).unsqueeze(3).broadcast_to([P, T, HEADS, HD]), ALU.mult)
                        last.then_inc(kvz_ok, 1)
                    for u in LANES:
                        dve.wait_ge(au_ps, lap[u])
                        V.tensor_scalar(den[u][:, :, :], bank[u][2][:, 0:2 * S].rearrange("p (f n) -> p f n", f=2),
                                        EPS_K, None, ALU.add).then_inc(den_a, 1)
                    for u in LANES:
                        dve.wait_ge(den_a, lap[u])
                        V.reciprocal(den[u][:, :, :], den[u][:, :, :]).then_inc(den_b, 1)
                    for u in LANES:
                        dve.wait_ge(den_b, lap[u])
                        for half in range(2):
                            last = V.tensor_tensor(
                                sq[u][:, half, :].rearrange("p (n e) -> p n e", e=HD),
                                bank[u][1 - half][:, :].rearrange("p (e n) -> p n e", e=HD),
                                den[u][:, half, :].unsqueeze(2).broadcast_to([P, S, HD]), ALU.mult)
                        last.then_inc(att_ok, 1)
                    for u in LANES:
                        dve.wait_ge(o2_ok, lap[u])
                        V.tensor_reduce(ss[u][:, 0:T], t4(sq[u][:, 0, :]), AX.X, ALU.add).then_inc(y_b, 1)
                    for u in LANES:
                        dve.wait_ge(y_b, lap[u])
                        V.tensor_scalar(ve2[u][:, :], ss[u][:, 0:T], 1.0 / D, EPS_A, ALU.mult, ALU.add).then_inc(oss_ok, 1)
                    for u in LANES:
                        dve.wait_ge(o_rstd, lap[u])
                        for t in range(T):
                            last = V.scalar_tensor_tensor(out=x1[u][:, t, :], in0=t4(bank[u][3][:, :])[:, t, :],
                                                          scalar=rs2[u][:, t:t + 1], in1=gamma_b[:, :],
                                                          op0=ALU.mult, op1=ALU.mult)
                        last.then_inc(og_ok, 1)
                    for u in LANES:
                        dve.wait_ge(og_ok, lap[u])
                        dve.wait_ge(xpb_ok, lap[u])
                        V.tensor_tensor(x1[u][:, :, :], x1[u][:, :, :], xpb[u][:, :, :], ALU.add).then_inc(x1_ok, 1)
                    for u in LANES:
                        dve.wait_ge(x1_ok, lap[u])
                        moments(x1[u], u, a_b, z_var, EPS_X, lap[u])
                    for u in LANES:
                        dve.wait_ge(z_rstd, lap[u])
                        normalize(zed[u], x1[u], u).then_inc(z_ok, 1)
                    for u in LANES:
                        dve.wait_ge(z_ok, lap[u])
                        dve.wait_ge(h_rstd, lap[u])
                        V.tensor_tensor(xn[u][:, :, :], zed[u][:, :, :], over_d(rs[u][:, 0:T]), ALU.mult).then_inc(h_ok, 1)
                    for u in LANES:
                        dve.wait_ge(qf_ps, lap[u])
                        for b in range(BPT):
                            rows = slice(b * S, b * S + S)
                            for gg in range(2):
                                last = V.tensor_scalar(
                                    qbd[u][rows, gg, :, b * S:b * S + S],
                                    bank[u][1][rows, gg * T * S:(gg + 1) * T * S].rearrange("p (t s) -> p t s", t=T),
                                    bq_cols[rows, gg:gg + 1], SCALE, ALU.add, ALU.mult)
                        last.then_inc(qbd_ok, 1)
                        dve.wait_ge(kf_ok, lap[u])
                        for gg in range(2):
                            for h in range(HG):
                                last = V.tensor_scalar(km[u][:, gg, h, :], kb[u][:, gg, :], head8[:, h:h + 1], None,
                                                       ALU.mult)
                        last.then_inc(km_ok, 1)
                        dve.wait_ge(vf_ps, lap[u])
                        for odd in range(2):
                            rows = slice(odd * S, odd * S + S)
                            last = V.tensor_tensor(
                                vbd[u][rows, :, :, odd * (HD + 1):odd * (HD + 1) + HD],
                                bank[u][3][rows, :].rearrange("p (t h d) -> p t h d", h=HG, d=HD),
                                bv_b[rows, :].rearrange("p (h d) -> p h d", h=HG).unsqueeze(1)
                                .broadcast_to([S, T * BPT, HG, HD]), ALU.add)
                        last.then_inc(vbd_ok, 1)
                    for n in range(UNITS + 1):
                        for u in LANES:
                            if n < UNITS:
                                dve.wait_ge(s_ps, (g * UNITS) + 2 * n + u + 1)
                                if n >= 2:
                                    dve.wait_ge(sm_ps, (g * UNITS) + 2 * (n - 2) + u + 1)
                                V.tensor_reduce(mx[u][:, n % 2, :],
                                                bank[u][n % 2][:, :].rearrange("p (h k) -> p h k", h=HG),
                                                AX.X, ALU.max).then_inc(mx_ok, 1)
                        if n >= 2 and n % 2 == 0:
                            t = n // 2 - 1
                            for u in LANES:
                                pv = bank[u][3][:, 0:HG * 4 * (HD + 1)].rearrange(
                                    "p (h b o c) -> p h b o c", h=HG, b=BPT, o=2)
                                dve.wait_ge(pv_ps, (g * UNITS) + 2 * (n - 1) + u + 1)
                                V.reciprocal(rden[u][:, :].rearrange("p (h o) -> p h o", o=2),
                                             pv[:, :, 0, :, HD]).then_inc(rden_ok, 1)
                            for u in LANES:
                                pv = bank[u][3][:, 0:HG * 4 * (HD + 1)].rearrange(
                                    "p (h b o c) -> p h b o c", h=HG, b=BPT, o=2)
                                dve.wait_ge(rden_ok, (g * T) + 2 * t + u + 1)
                                for b in range(BPT):
                                    rows = slice(b * S, b * S + S)
                                    last = V.tensor_tensor(
                                        xn[u][rows, t, :].rearrange("p (h o d) -> p h o d", h=HG, o=2),
                                        pv[rows, :, b, :, 0:HD],
                                        rden[u][rows, :].rearrange("p (h o) -> p h o", o=2).unsqueeze(3)
                                        .broadcast_to([S, HG, 2, HD]), ALU.mult)
                                last.then_inc(y_ok, 1)
                    for u in LANES:
                        dve.wait_ge(f_ps, lap[u])
                        V.tensor_tensor(x_sb[u][:, :, :], t4(bank[u][1][:, :]), zed[u][:, :, :], ALU.add).then_inc(xa_ok, 1)
                    for u in LANES:
                        dve.wait_ge(xa_ok, lap[u])
                        moments(x_sb[u], u, topi_ok, a_var, EPS_X, lap[u])
                    for u in LANES:
                        dve.wait_ge(a_rstd, lap[u])
                        normalize(xn[u], x_sb[u], u).then_inc(a_ok, 1)
                    for u in LANES:
                        dve.wait_ge(lg_ps, lap[u])
                        V.tensor_copy(hot[u][:, 0, :, :], bank[u][3][:, 0:T * E].rearrange("p (t e) -> p t e", t=T))
                    for u in LANES:
                        if u == LANES[0]:
                            dve.drain()
                        for t in range(T):
                            last = V.max(top[u][:, t, :], hot[u][:, 0, t, :])
                        last.then_inc(top_ok, 1)
                    for u in LANES:
                        dve.wait_ge(top_ok, lap[u])
                        V.tensor_tensor(dlt[u][:, :], top[u][:, :, 1], top[u][:, :, 0], ALU.subtract).then_inc(dl_ok, 1)
                        for t in range(T):
                            last = V.max_index(topi[u][:, t, :], top[u][:, t, :], hot[u][:, 0, t, :])
                        last.then_inc(w2_ok, 1)
                    for u in LANES:
                        dve.wait_ge(w2_ok, lap[u])
                        V.tensor_copy(topf[u][:, :, :], topi[u][:, :, 0:2]).then_inc(hot_a, 1)
                        dve.wait_ge(e_ok, lap[u])
                        V.tensor_scalar(wgt[u][:, 1, :], dlt[u][:, :], 1.0, None, ALU.add).then_inc(w1_ok, 1)
                        dve.wait_ge(w1_ok, lap[u] + 2)
                        V.reciprocal(wgt[u][:, 0, :], wgt[u][:, 1, :]).then_inc(winv_ok, 1)
                        dve.wait_ge(winv_ok, lap[u])
                        V.tensor_tensor(wgt[u][:, 1, :], wgt[u][:, 0, :], dlt[u][:, :], ALU.mult).then_inc(wpair_ok, 1)
                    for u in LANES:
                        dve.wait_ge(hot_a, lap[u])
                        for k in range(2):
                            last = V.tensor_tensor(hot[u][:, k, :, :], iota8[:, :].unsqueeze(1).broadcast_to([P, T, E]),
                                                   topf[u][:, :, k:k + 1].broadcast_to([P, T, E]), ALU.is_equal)
                        last.then_inc(hot_b, 1)
                    for u in LANES:
                        dve.wait_ge(hot_b, lap[u])
                        dve.wait_ge(wpair_ok, lap[u])
                        V.tensor_tensor(hot[u][:, :, :, :].rearrange("p k t e -> p (k t) e"),
                                        hot[u][:, :, :, :].rearrange("p k t e -> p (k t) e"),
                                        wgt[u][:, :, :].rearrange("p k t -> p (k t)").unsqueeze(2)
                                        .broadcast_to([P, 2 * T, E]), ALU.mult).then_inc(hotw_ok, 1)
                    for u in LANES:
                        dve.wait_ge(hotw_ok, lap[u])
                        V.tensor_tensor(gate[:, g + u, :, :], hot[u][:, 0, :, :], hot[u][:, 1, :, :], ALU.add).then_inc(gate_ok, 1)

                V.memset(w8[0][:, 0, 0:1], 0.0).then_inc(acc_ok, 2)
                dve.wait_ge(res_ok, GROUPS)
                with dve.Fori(0, E // 2) as rep:
                    for e in range(2):
                        with dve.Fori(0, GROUPS // 2) as r:
                            for u in LANES:
                                item = (rep * 2 + e) * GROUPS + r * 2 + u
                                dve.wait_ge(y2_ps, item + 1)
                                for t in range(T):
                                    last = V.scalar_tensor_tensor(
                                        out=acc[:, r * 2 + u, t, :], in0=t4(bank[u][2][:, :])[:, t, :],
                                        scalar=gate[:, r * 2 + u, t, bass.ts(rep * 2 + e, 1)],
                                        in1=acc[:, r * 2 + u, t, :], op0=ALU.mult, op1=ALU.add)
                                last.then_inc(acc_ok, 1)



_INS = ['x', 'ctx_1024', 'mask_BxS2_ff1', 'L0_xattn_wq', 'L0_xattn_wk', 'L0_xattn_wv', 'L0_xattn_ln_gamma',
        'L0_xattn_ln_beta', 'L0_xattn_dense_w', 'L0_xattn_dense_b', 'L0_ffn_ln1_g', 'L0_ffn_ln1_b', 'L0_ffn_ln2_g',
        'L0_ffn_ln2_b', 'L0_ffn_Wq', 'L0_ffn_bq', 'L0_ffn_Wk', 'L0_ffn_bk', 'L0_ffn_Wv', 'L0_ffn_bv', 'L0_ffn_Wp',
        'L0_ffn_bp', 'L0_ffn_gate_W', 'L0_ffn_gate_b', 'L0_ffn_exp_W1', 'L0_ffn_exp_b1', 'L0_ffn_exp_W2',
        'L0_ffn_exp_b2']


def kernel(**inputs):
    import numpy as _np
    import concourse.bacc as _bacc
    from concourse import mybir as _mybir
    from concourse.bass_utils import run_bass_kernel_spmd as _run

    nc = _bacc.Bacc("TRN2", target_bir_lowering=False, num_devices=1)
    arrays, args = {}, {}
    for name in _INS:
        arr = _np.ascontiguousarray(inputs[name])
        arrays[f"in_{name}_dram"] = arr
        args[name] = nc.dram_tensor(f"in_{name}_dram", arr.shape, _mybir.dt.from_np(arr.dtype), kind="ExternalInput").ap()
    out = nc.dram_tensor("out_0_dram", (64, 64, 128), _mybir.dt.float32, kind="ExternalOutput").ap()
    xattn_attention_moe(nc, args, out)
    r = _run(nc, [arrays], core_ids=[0])
    return r.results[0]["out_0_dram"]
```

```python
from contextlib import ExitStack

import concourse.bass as bass
from concourse import mybir

ALU = mybir.AluOpType
ACT = mybir.ActivationFunctionType
AX = mybir.AxisListType
F32 = mybir.dt.float32
F32R = mybir.dt.float32r
BF16 = mybir.dt.bfloat16
U32 = mybir.dt.uint32

P = 128
LANES = (0, 1)
EPS_X = 1e-5
EPS_K = 1e-6
EPS_A = 1e-6
MASKED = -1e30


def xattn_attention_moe(nc: bass.Bass, a, out):
    B, S, D = a["x"].shape
    HEADS = 16
    HD = D // HEADS
    TILES = B * S // P
    T = 4
    N = T * P
    GROUPS = TILES // T
    E, _, H = a["L0_ffn_exp_W1"].shape
    CH = H // P
    BPT = P // S
    HG = HEADS // 2
    UNITS = 2 * T
    SCALE = float(HD) ** -0.5
    assert D == P and BPT == 2 and HG * S == 512

    x_v = a["x"].rearrange("(g t b) s d -> g (b s) t d", t=T, b=BPT)
    ctx_v = a["ctx_1024"].rearrange("(g t b) s d -> g (b s) t d", t=T, b=BPT)
    w2_v = a["L0_ffn_exp_W2"].rearrange("e (c p) d -> e p c d", p=P)
    b1_v = a["L0_ffn_exp_b1"].rearrange("e (c p o) -> e c p o", p=P, o=1)
    em_v = a["mask_BxS2_ff1"].rearrange("(g t b) s -> g (b s) t", t=T, b=BPT)
    out_v = out.rearrange("(g t b) s d -> g (b s) t d", t=T, b=BPT)

    with ExitStack() as ctx:
        def sb(name, shape, dt=F32):
            return ctx.enter_context(nc.sbuf_tensor(name, shape, dt))

        def lanes(name, shape, dt=F32):
            return [sb(f"{name}{u}", shape, dt) for u in LANES]

        def sems(names):
            return [ctx.enter_context(nc.semaphore(n)) for n in names.split()]

        bank = [ctx.enter_context(nc.psum_tensor(f"bank{k}", [P, 512], F32)) for k in range(8)]
        score_bank, probT_bank, pv_bank, front_bank, end_bank = bank[0:2], bank[2], bank[3], bank[4:7], bank[7]

        ident = sb("ident", [P, P])
        ident_bf = sb("ident_bf", [P, P], BF16)
        neg_ident = sb("neg_ident", [P, P], F32R)
        causal = sb("causal", [P, S], BF16)
        head16 = sb("head16", [P, HEADS])
        head8 = sb("head8", [P, HG])
        batch2 = sb("batch2", [P, BPT])
        minus_half = sb("minus_half", [P, 3 * T])
        ones_row = sb("ones_row", [1, P])
        ones_r = sb("ones_r", [1, P], F32R)
        iota8 = sb("iota8", [P, E])
        w_raw = sb("w_raw", [P, 4, D])
        w_sum = sb("w_sum", [P, 4])
        wx = sb("wx", [P, 4, D])
        db_raw = sb("db_raw", [1, D])
        db_sum = sb("db_sum", [1, 1])
        db_row = sb("db_row", [1, D])
        db_hi = sb("db_hi", [1, D], F32R)
        db_lo = sb("db_lo", [1, D], F32R)
        wf = sb("wf", [P, 4, D])
        gate_w = sb("gate_w", [P, E])
        gamma_b = sb("gamma_b", [P, D])
        beta_b = sb("beta_b", [P, D])
        bv_b = sb("bv_b", [P, D])
        bp_b = sb("bp_b", [P, D])
        cols = sb("cols", [P, 8])
        gb_row = sb("gb_row", [1, E])

        x_sb = lanes("x_sb", [P, T, D])
        c_sb = lanes("c_sb", [P, T, D])
        em = lanes("em", [P, T])
        em2 = sb("em2", [P, T])
        emb = sb("emb", [P, T, BPT])
        stats = sb("stats", [P, T, 6])
        mv = sb("mv", [P, T, 2])
        x_ve = sb("x_ve", [P, T])
        x_rs = sb("x_rs", [P, T])
        x1_stats = sb("x1_stats", [P, T, 6])
        x1_mv = sb("x1_mv", [P, T, 2])
        hn = sb("hn", [P, T, D])
        ve = sb("ve", [P, 3 * T])
        rs = sb("rs", [P, 3 * T])
        rinv = sb("rinv", [P, T])
        rprod = sb("rprod", [P, T])
        ss = sb("ss", [P, 3 * T])
        sq = sb("sq", [P, 3, N])
        xn = sb("xn", [P, T, D])
        xpb = sb("xpb", [P, T, D])
        xnT = sb("xnT", [P, N])
        cT = sb("cT", [P, N])
        qn = sb("qn", [P, T, D])
        qp = sb("qp", [P, N])
        kp = sb("kp", [P, T, D])
        vp = sb("vp", [P, T, D])
        kvz = sb("kvz", [P, T, BPT, HD + 1, 32])
        den = sb("den", [P, 2, S])
        att = sb("att", [P, 2, N])
        zed = lanes("zed", [P, T, D])
        x1 = lanes("x1", [P, T, D])
        h1T = sb("h1T", [P, T, P])
        kb = lanes("kb", [P, 2, T * S])

        qbd = lanes("qbd", [P, 2, T, P])
        km = lanes("km", [P, HG, S])
        vbd = lanes("vbd", [P, T, BPT, HG, 2 * (HD + 1)])
        mx = sb("mx", [P, 2, HG], F32R)
        pr = sb("pr", [P, 2, 512])
        pT = sb("pT", [P, 4, P])
        rden = sb("rden", [P, HEADS])
        y = lanes("y", [P, T, D])

        yT = sb("yT", [P, N])
        xa = sb("xa", [P, T, D])
        e_stats = sb("e_stats", [P, T, 6])
        e_mv = sb("e_mv", [P, T, 2])
        e_ve = sb("e_ve", [P, T])
        e_rs = sb("e_rs", [P, T])
        an = sb("an", [P, T, D])
        hgT = sb("hgT", [P, T, P])
        logits = sb("logits", [P, T, E])
        top = sb("top", [P, T, 8])
        topi = sb("topi", [P, T, 8], U32)
        topf = sb("topf", [P, T, 2])
        dlt = sb("dlt", [P, T])
        wgt = sb("wgt", [P, 3, T])
        hot = sb("hot", [P, 2, T, E])

        h2T = sb("h2T", [P, GROUPS, N])
        acc = sb("acc", [P, GROUPS, T, D])
        gate = sb("gate", [P, GROUPS, T, E])

        w1 = [sb(f"w1_{e}", [P, H]) for e in range(2)]
        w2 = [sb(f"w2_{e}", [P, CH, D]) for e in range(2)]
        b1 = [sb(f"b1_{e}", [P, CH]) for e in range(2)]
        b2 = [sb(f"b2_{e}", [1, D]) for e in range(2)]
        mid = lanes("mid", [P, CH, N])

        (w_loaded, cT_ps, em2_ok, emb_ok, xpb_ok, xn_ok, y2_ps, acc_ok, stored, xT_ok, lg_ok, cT_ok, xT_ps,
         kf_ok, qbd_ok, vbd_ok, k_ps, v_ps, q_ps, qn_ok, qT_ps, kp_ok, vn_ok, ks_ps, vp_ok, qr_ok, kv_ps,
         kvz_ok, qp_ok, au_ps, att_ok, aT_ps, aT_ok, o_ps, h_ok, hT_ps, hT_ok, kf_ps, qf_ps, vf_ps, km0_ok,
         km_ok, s_ps, mx_ok, sm_ps, p_ok, pT_ps, pT_ok, y_ok, pv_ps, yT_ps, yT_ok, f_ps, a_ok, aT2_ps, h2T_ok,
         lg_ps, consts, w_ready, gate_ok, mid_ok, mid_ps, sq_ok, o2_ok, dl_ok, e_ok, setup, x_var, x_rstd,
         x1_ok, ss_ok, qkv_rstd, vg_ok, vb_ok, oss_ok, o_rstd, z_var, z_rstd, z_ok, zb_ok, a_var, a_rstd,
         xa_ok, res_ok, xs_b, sum_ok, kn_ok, kg_ok, kb_ok, den_a, den_b, osum_ok, og_ok, zs_b, zv_a, zv_b,
         zv_c, rp_ok, rden_ok, as_b, kept_ok, top_ok, topi_ok, hot_a, wsum_ok, hot_b, winv_ok, wpair_ok,
         hotw_ok, zeroed, centred) = sems(
            "w_loaded cT_ps em2_ok emb_ok xpb_ok xn_ok y2_ps acc_ok stored xT_ok lg_ok cT_ok xT_ps kf_ok "
            "qbd_ok vbd_ok k_ps v_ps q_ps qn_ok qT_ps kp_ok vn_ok ks_ps vp_ok qr_ok kv_ps kvz_ok qp_ok au_ps "
            "att_ok aT_ps aT_ok o_ps h_ok hT_ps hT_ok kf_ps qf_ps vf_ps km0_ok km_ok s_ps mx_ok sm_ps p_ok "
            "pT_ps pT_ok y_ok pv_ps yT_ps yT_ok f_ps a_ok aT2_ps h2T_ok lg_ps consts w_ready gate_ok mid_ok "
            "mid_ps sq_ok o2_ok dl_ok e_ok setup x_var x_rstd x1_ok ss_ok qkv_rstd vg_ok vb_ok oss_ok o_rstd "
            "z_var z_rstd z_ok zb_ok a_var a_rstd xa_ok res_ok xs_b sum_ok kn_ok kg_ok kb_ok den_a den_b "
            "osum_ok og_ok zs_b zv_a zv_b zv_c rp_ok rden_ok as_b kept_ok top_ok topi_ok hot_a wsum_ok hot_b "
            "winv_ok wpair_ok hotw_ok zeroed centred")
        c_loaded = sems("c_loaded0 c_loaded1")
        x_loaded = sems("x_loaded0 x_loaded1")
        m_loaded = sems("m_loaded0 m_loaded1")
        w1_loaded = sems("w1_loaded0 w1_loaded1")
        w2_loaded = sems("w2_loaded0 w2_loaded1")
        b2_loaded = sems("b2_loaded0 b2_loaded1")
        b1_loaded = sems("b1_loaded0 b1_loaded1")

        def col(v):
            return v.rearrange("(p o) -> p o", o=1)

        def row(v):
            return v.rearrange("(o n) -> o n", o=1)

        def t4(ap):
            return ap.rearrange("p (t d) -> p t d", t=T)

        def over_d(ap):
            return ap.unsqueeze(2).broadcast_to([P, ap.shape[1], D])

        def over_t(ap):
            return ap.unsqueeze(1).broadcast_to([ap.shape[0], T, ap.shape[1]])

        def half(b):
            return slice(b * S, b * S + S)

        G1, B1, G2, B2, BQ, BK, GX, BX = (slice(i, i + 1) for i in range(8))
        weights = [
            (w_raw[:, 0, :], a["L0_xattn_wq"]), (w_raw[:, 1, :], a["L0_xattn_wk"]),
            (w_raw[:, 2, :], a["L0_xattn_wv"]), (w_raw[:, 3, :], a["L0_xattn_dense_w"]),
            (db_raw[:, :], row(a["L0_xattn_dense_b"])),
            (gamma_b[:, :], row(a["L0_xattn_ln_gamma"]).broadcast_to([P, D])),
            (beta_b[:, :], row(a["L0_xattn_ln_beta"]).broadcast_to([P, D])),
            (cols[:, GX], col(a["L0_xattn_ln_gamma"])), (cols[:, BX], col(a["L0_xattn_ln_beta"])),
            (wf[:, 0, :], a["L0_ffn_Wq"]), (wf[:, 1, :], a["L0_ffn_Wk"]), (wf[:, 2, :], a["L0_ffn_Wv"]),
            (wf[:, 3, :], a["L0_ffn_Wp"]), (gate_w[:, :], a["L0_ffn_gate_W"]),
            (bv_b[:, :], row(a["L0_ffn_bv"]).broadcast_to([P, D])),
            (bp_b[:, :], row(a["L0_ffn_bp"]).broadcast_to([P, D])),
            (cols[:, G1], col(a["L0_ffn_ln1_g"])), (cols[:, B1], col(a["L0_ffn_ln1_b"])),
            (cols[:, G2], col(a["L0_ffn_ln2_g"])), (cols[:, B2], col(a["L0_ffn_ln2_b"])),
            (cols[:, BQ], col(a["L0_ffn_bq"])), (cols[:, BK], col(a["L0_ffn_bk"])),
            (gb_row[:, :], row(a["L0_ffn_gate_b"])),
        ]

        def schedule(eng, opening, front, slot, finish):
            def beat(k, u, first=False):
                nxt = None if isinstance(k, int) and k + 1 >= GROUPS else (k + 1, 1 - u)
                later = None if isinstance(k, int) and k + 2 >= GROUPS else (k + 2, u)
                prev = None if first else (k - 1, 1 - u)
                for n in range(UNITS):
                    slot(n, (k, u), nxt, later, prev)

            opening(0, 0)
            front(0, 0)
            opening(1, 1)
            beat(0, 0, first=True)
            with eng.Fori(0, GROUPS // 2 - 2) as r:
                beat(2 * r + 1, 1)
                beat(2 * r + 2, 0)
            for k in range(GROUPS - 3, GROUPS):
                beat(k, k % 2)
            finish(GROUPS - 1, 1)

        with nc.Block() as block:
            @block.sync
            def _(sp):
                for dst, src in weights:
                    sp.dma_start(dst, src).then_inc(w_loaded, 16)

                def load(u, group):
                    sp.dma_start(c_sb[u][:, :, :], ctx_v[group]).then_inc(c_loaded[u], 16)
                    sp.dma_start(x_sb[u][:, :, :], x_v[group]).then_inc(x_loaded[u], 16)
                    sp.dma_start(em[u][:, :], em_v[group], allow_slow_non_contiguous=True).then_inc(m_loaded[u], 16)

                for u in LANES:
                    load(u, u)

                def load_expert(e, expert):
                    sp.dma_start(w1[e][:, :], a["L0_ffn_exp_W1"][expert]).then_inc(w1_loaded[e], 16)
                    sp.dma_start(w2[e][:, :, :], w2_v[expert]).then_inc(w2_loaded[e], 16)
                    sp.dma_start(b2[e][:, :], a["L0_ffn_exp_b2"].rearrange("e (o d) -> e o d", o=1)[expert])\
                      .then_inc(b2_loaded[e], 16)
                    for c in range(CH):
                        sp.dma_start(b1[e][:, c:c + 1], b1_v[expert][c]).then_inc(b1_loaded[e], 16)

                for e in range(2):
                    load_expert(e, e)
                with sp.Fori(0, GROUPS // 2 - 1) as r:
                    for u in LANES:
                        k = 2 * r + u
                        sp.wait_ge(cT_ps, k + 1)
                        sp.wait_ge(em2_ok, k + 1)
                        sp.wait_ge(emb_ok, k + 1)
                        sp.wait_ge(xpb_ok, k + 1)
                        sp.wait_ge(xn_ok, k + 1)
                        load(u, k + 2)
                with sp.Fori(0, E // 2 - 1) as rep:
                    for e in range(2):
                        sp.wait_ge(y2_ps, (rep * 2 + e + 1) * GROUPS)
                        load_expert(e, rep * 2 + e + 2)
                for g in range(GROUPS):
                    sp.wait_ge(acc_ok, (E - 1) * GROUPS + g + 3)
                    sp.dma_start(out_v[g], acc[:, g, :, :]).then_inc(stored, 16)
                sp.wait_ge(stored, 16 * GROUPS)

            @block.tensor
            def _(pe):
                F0, F1, F2 = front_bank

                def per_tile(psum, lhsT, rhs):
                    for t in range(T):
                        last = pe.matmul(t4(psum[:, :])[:, t, :], lhsT[:, t * P:t * P + P], rhs, start=True, stop=True)
                    return last

                def transposes(psum, src):
                    for t in range(T):
                        last = pe.transpose(t4(psum[:, :])[:, t, :], src[:, t, :], ident[:, :])
                    return last

                def context_T(k, u):
                    pe.wait_ge(c_loaded[u], (k // 2 + 1) * 16)
                    if isinstance(k, int) and k == 1:
                        pe.wait_ge(xT_ok, 1)
                    elif not (isinstance(k, int) and k < 3):
                        pe.wait_ge(lg_ok, k - 2)
                    transposes(end_bank, c_sb[u]).then_inc(cT_ps, 1)

                def x_T(k):
                    pe.wait_ge(xn_ok, k + 1)
                    pe.wait_ge(cT_ok, k + 1)
                    transposes(end_bank, xn).then_inc(xT_ps, 1)

                def project_kv(k):
                    pe.wait_ge(cT_ok, k + 1)
                    if not (isinstance(k, int) and k == 0):
                        pe.wait_ge(kf_ok, k)
                        pe.wait_ge(qbd_ok, k)
                        pe.wait_ge(vbd_ok, k)
                    per_tile(F1, cT, wx[:, 1, :]).then_inc(k_ps, 1)
                    pe.wait_ge(xT_ok, k + 1)
                    per_tile(F0, cT, wx[:, 2, :]).then_inc(v_ps, 1)

                def project_q(k):
                    per_tile(F2, xnT, wx[:, 0, :]).then_inc(q_ps, 1)

                def q_T(k):
                    pe.wait_ge(qn_ok, k + 1)
                    transposes(F2, qn).then_inc(qT_ps, 1)

                def key_sums(k):
                    pe.wait_ge(kp_ok, k + 1)
                    pe.wait_ge(emb_ok, k + 1)
                    pe.wait_ge(vn_ok, k + 1)
                    for t in range(T):
                        last = pe.matmul(F0[:, t * BPT:t * BPT + BPT], kp[:, t, :], emb[:, t, :], start=True, stop=True)
                    last.then_inc(ks_ps, 1)

                def key_values(k):
                    pe.wait_ge(vp_ok, k + 1)
                    pe.wait_ge(qr_ok, k + 1)
                    for b in range(BPT):
                        for t in range(T):
                            last = pe.matmul(t4(front_bank[1 + b][:, :])[:, t, :], kp[half(b), t, :],
                                             vp[half(b), t, :], start=True, stop=True)
                    last.then_inc(kv_ps, 1)

                def linear_attention(k, part):
                    if part == 0:
                        pe.wait_ge(kvz_ok, k + 1)
                        pe.wait_ge(qp_ok, k + 1)
                    for c in range(HD + 1):
                        dst, at = (front_bank[part], c * S) if c < HD else (F2, part * S)
                        for b4 in range(4):
                            t, b = 2 * part + b4 // 2, b4 % 2
                            last = pe.matmul(dst[b4 * 32:b4 * 32 + 32, at:at + S], kvz[:, t, b, c, :],
                                             qp[:, t * P + b * S:t * P + b * S + S], start=True, stop=True)
                    last.then_inc(au_ps, 1)

                def attention_T(k):
                    pe.wait_ge(att_ok, k + 1)
                    for part in range(2):
                        for n4 in range(4):
                            last = pe.transpose((F2, F0)[part][:, n4 * P:n4 * P + P],
                                                att[:, part, n4 * P:n4 * P + P], ident[:, :])
                    last.then_inc(aT_ps, 1)

                def dense(k):
                    pe.wait_ge(aT_ok, k + 1)
                    pe.matmul(t4(F1[:, :]), ones_r[:, :], over_t(db_hi[:, :]), start=True, stop=True)
                    pe.matmul(t4(F1[:, :]), ones_r[:, :], over_t(db_lo[:, :]), start=False, stop=True,
                              skip_group_check=True)
                    for t in range(T):
                        last = pe.matmul(t4(F1[:, :])[:, t, :], xnT[:, t * P:t * P + P], wx[:, 3, :],
                                         start=False, stop=True, skip_group_check=True)
                    last.then_inc(o_ps, 1)

                def h_T(k):
                    pe.wait_ge(h_ok, k + 1)
                    transposes(F0, hn).then_inc(hT_ps, 1)

                def project_self(k):
                    pe.wait_ge(hT_ok, k + 1)
                    h = h1T[:, :, :].rearrange("p t n -> p (t n)")
                    pe.matmul(F1[:, :], wf[:, 1, :], h, start=True, stop=True).then_inc(kf_ps, 1)
                    pe.matmul(F2[:, :], wf[:, 0, :], h, start=True, stop=True).then_inc(qf_ps, 1)
                    per_tile(F0, h, wf[:, 2, :]).then_inc(vf_ps, 1)

                def scores(k, u, n):
                    if n == 0:
                        pe.wait_ge(qbd_ok, k + 1)
                        pe.wait_ge(km0_ok, k + 1)
                    else:
                        pe.wait_ge(km_ok, k * (UNITS - 1) + n)
                    bank_n = score_bank[n % 2]
                    pe.matmul(bank_n[:, :], ident_bf[:, :], causal[:, :].unsqueeze(1).broadcast_to([P, HG, S]),
                              start=True, stop=False)
                    pe.matmul(bank_n[:, :], qbd[u][:, n % 2, n // 2, :], km[n % 2][:, :, :],
                              start=False, stop=True).then_inc(s_ps, 1)

                def subtract_max(k, n):
                    pe.wait_ge(mx_ok, k * UNITS + (n + 1))
                    pe.matmul(score_bank[n % 2][:, :], neg_ident[:, :],
                              mx[:, n % 2, :].unsqueeze(2).broadcast_to([P, HG, S]),
                              start=False, stop=True, skip_group_check=True).then_inc(sm_ps, 1)

                def probs_T(k, n):
                    pe.wait_ge(p_ok, k * UNITS + (n + 1))
                    for j in range(4):
                        last = pe.transpose(probT_bank[:, j * P:j * P + P], pr[:, n % 2, j * P:j * P + P], ident[:, :])
                    last.then_inc(pT_ps, 1)

                def probs_values(k, u, n):
                    t = n // 2
                    pe.wait_ge(pT_ok, k * UNITS + (n + 1))
                    if n == 0:
                        pe.wait_ge(vbd_ok, k + 1)
                    if n % 2 == 0 and not (isinstance(k, int) and k * T + t == 0):
                        pe.wait_ge(y_ok, k * T + t)
                    W = 2 * BPT * (HD + 1)
                    for j in range(4):
                        hp = (n % 2) * 4 + j
                        last = pe.matmul(pv_bank[:, hp * W:hp * W + W].rearrange("p (b c) -> p b c", b=BPT),
                                         pT[:, j, :], vbd[u][:, t, :, hp, :], start=True, stop=True)
                    last.then_inc(pv_ps, 1)

                def y_T(k, u):
                    pe.wait_ge(y_ok, (k + 1) * T)
                    opened = k + 3
                    pe.wait_ge(xT_ok, min(opened, GROUPS) if isinstance(k, int) else opened)
                    if not (isinstance(k, int) and k == 0):
                        pe.wait_ge(lg_ok, k)
                    transposes(end_bank, y[u]).then_inc(yT_ps, 1)

                def project_out(k):
                    pe.wait_ge(yT_ok, k + 1)
                    per_tile(end_bank, yT, wf[:, 3, :]).then_inc(f_ps, 1)

                def a_T(k):
                    pe.wait_ge(a_ok, k + 1)
                    transposes(end_bank, an).then_inc(aT2_ps, 1)

                def gate_logits(k):
                    pe.wait_ge(h2T_ok, k + 1)
                    lg = end_bank[:, 0:T * E].rearrange("p (t e) -> p t e", t=T)
                    pe.matmul(lg, ones_row[:, :], over_t(gb_row[:, :]), start=True, stop=True)
                    for t in range(T):
                        last = pe.matmul(lg[:, t, :], hgT[:, t, :], gate_w[:, :], start=False, stop=True,
                                         skip_group_check=True)
                    last.then_inc(lg_ps, 1)

                def opening(k, u):
                    context_T(k, u)
                    x_T(k)

                def front(k, u):
                    project_kv(k)
                    project_q(k)
                    q_T(k)
                    key_sums(k)
                    key_values(k)
                    linear_attention(k, 0)
                    linear_attention(k, 1)
                    attention_T(k)
                    dense(k)
                    h_T(k)
                    project_self(k)

                def slot(n, unit, nxt, later, prev):
                    k, u = unit
                    if n == 0:
                        scores(k, u, 0)
                    subtract_max(k, n)
                    if n + 1 < UNITS:
                        if not (isinstance(k, int) and k * UNITS + n == 0):
                            pe.wait_ge(p_ok, k * UNITS + n)
                        scores(k, u, n + 1)
                    if prev:
                        if n == 0:
                            y_T(*prev)
                        if n == 1:
                            project_out(prev[0])
                        if n == 4:
                            a_T(prev[0])
                    if nxt:
                        if n == 0:
                            project_kv(nxt[0])
                        if n == 3:
                            key_sums(nxt[0])
                        if n == 4:
                            linear_attention(nxt[0], 0)
                        if n == 5:
                            attention_T(nxt[0])
                    if later:
                        if n == 6:
                            context_T(*later)
                        if n == 7:
                            x_T(later[0])
                    probs_T(k, n)
                    if nxt:
                        if n == 0:
                            project_q(nxt[0])
                        if n == 2:
                            q_T(nxt[0])
                        if n == 3:
                            key_values(nxt[0])
                        if n == 4:
                            linear_attention(nxt[0], 1)
                        if n == 5:
                            dense(nxt[0])
                        if n == 7:
                            h_T(nxt[0])
                    if prev and n == 4:
                        gate_logits(prev[0])
                    probs_values(k, u, n)
                    if nxt and n == UNITS - 1:
                        project_self(nxt[0])

                def finish(k, u):
                    y_T(k, u)
                    project_out(k)
                    a_T(k)
                    gate_logits(k)

                pe.wait_ge(consts, 1)
                pe.wait_ge(w_ready, 1)
                schedule(pe, opening, front, slot, finish)

                pe.wait_ge(gate_ok, GROUPS)
                with pe.Fori(0, E // 2) as rep:
                    for e in range(2):
                        with pe.Fori(0, GROUPS // 2) as r:
                            pe.wait_ge(w1_loaded[e], (rep + 1) * 16)
                            pe.wait_ge(w2_loaded[e], (rep + 1) * 16)
                            pe.wait_ge(b2_loaded[e], (rep + 1) * 16)
                            for u in LANES:
                                item = (rep * 2 + e) * GROUPS + r * 2 + u
                                out_bank = bank[4 * u + 2]
                                for c in range(CH + 1):
                                    if c < CH:
                                        if c >= 2:
                                            pe.wait_ge(mid_ok, item * CH + (c - 1))
                                        pe.matmul(bank[4 * u + c % 2][:, :], w1[e][:, c * P:c * P + P],
                                                  h2T[:, r * 2 + u, :], start=True, stop=True).then_inc(mid_ps, 1)
                                    if c == 0:
                                        pe.wait_ge(acc_ok, item + 1)
                                        pe.matmul(t4(out_bank[:, :]), ones_row[:, :], over_t(b2[e][:, :]),
                                                  start=True, stop=True)
                                    if c >= 1:
                                        pe.wait_ge(mid_ok, item * CH + c)
                                        for t in range(T):
                                            last = pe.matmul(t4(out_bank[:, :])[:, t, :],
                                                             mid[u][:, c - 1, t * P:t * P + P], w2[e][:, c - 1, :],
                                                             start=False, stop=True, skip_group_check=True)
                                last.then_inc(y2_ps, 1)

            @block.scalar
            def _(act):
                A = nc.scalar.activation
                F0, F1, F2 = front_bank

                def copy_cT(k):
                    act.wait_ge(cT_ps, k + 1)
                    if not (isinstance(k, int) and k == 0):
                        act.wait_ge(v_ps, k)
                    nc.scalar.copy(cT[:, :], end_bank[:, :]).then_inc(cT_ok, 1)

                def copy_xT(k):
                    act.wait_ge(xT_ps, k + 1)
                    if not (isinstance(k, int) and k == 0):
                        act.wait_ge(o_ps, k)
                    nc.scalar.copy(xnT[:, :], end_bank[:, :]).then_inc(xT_ok, 1)

                def squares(k):
                    for w, src, ready in ((1, F1, k_ps), (2, F0, v_ps), (0, F2, q_ps)):
                        act.wait_ge(ready, k + 1)
                        last = A(sq[:, w, :], src[:, :], ACT.Square)
                    last.then_inc(sq_ok, 1)

                def q_relu(k):
                    act.wait_ge(qT_ps, k + 1)
                    A(qp[:, :], F2[:, :], ACT.Relu, bias=cols[:, BX], scale=cols[:, GX]).then_inc(qr_ok, 1)

                def copy_aT(k):
                    act.wait_ge(aT_ps, k + 1)
                    for part in range(2):
                        last = nc.scalar.copy(
                            xnT[:, part * 256:part * 256 + 256].rearrange("p (b h n) -> p n b h", b=4, n=4),
                            (F2, F0)[part][:, :].rearrange("p (n b x h) -> p n b x h", n=4, b=4, x=2)[:, :, :, 0, :])
                    last.then_inc(aT_ok, 1)

                def square_o(k):
                    act.wait_ge(o_ps, k + 1)
                    A(sq[:, 0, :], F1[:, :], ACT.Square).then_inc(o2_ok, 1)

                def copy_hT(k):
                    act.wait_ge(hT_ps, k + 1)
                    A(h1T[:, :, :], t4(F0[:, :]), ACT.Identity, bias=cols[:, B1], scale=cols[:, G1]).then_inc(hT_ok, 1)

                def keys(k, u):
                    act.wait_ge(kf_ps, k + 1)
                    for g in range(2):
                        for b in range(BPT):
                            last = A(kb[u][half(b), g, :].rearrange("p (t s) -> p t s", t=T),
                                     F1[half(g), :].rearrange("p (t b s) -> p t b s", t=T, b=BPT)[:, :, b, :],
                                     ACT.Identity, bias=cols[half(g), BK])
                    last.then_inc(kf_ok, 1)

                def exp_scores(k, n):
                    act.wait_ge(sm_ps, k * UNITS + (n + 1))
                    A(pr[:, n % 2, :], score_bank[n % 2][:, :], ACT.Exp).then_inc(p_ok, 1)

                def copy_pT(k, n):
                    act.wait_ge(pT_ps, k * UNITS + (n + 1))
                    if not (isinstance(k, int) and k * UNITS + n == 0):
                        act.wait_ge(pv_ps, k * UNITS + n)
                    nc.scalar.copy(pT[:, :, :], probT_bank[:, :].rearrange("p (j q) -> p j q", j=4)).then_inc(pT_ok, 1)

                def copy_yT(k):
                    act.wait_ge(yT_ps, k + 1)
                    nc.scalar.copy(yT[:, :], end_bank[:, :]).then_inc(yT_ok, 1)

                def copy_h2T(k):
                    act.wait_ge(aT2_ps, k + 1)
                    A(hgT[:, :, :], t4(end_bank[:, :]), ACT.Identity, bias=cols[:, B2], scale=cols[:, G2])\
                        .then_inc(h2T_ok, 1)

                def exp_gap(k):
                    act.wait_ge(dl_ok, k + 1)
                    A(dlt[:, :], dlt[:, :], ACT.Exp).then_inc(e_ok, 1)

                def opening(k, u):
                    copy_cT(k)
                    copy_xT(k)

                def front(k, u):
                    squares(k)
                    q_relu(k)
                    copy_aT(k)
                    square_o(k)
                    copy_hT(k)
                    keys(k, u)

                def slot(n, unit, nxt, later, prev):
                    k, u = unit
                    exp_scores(k, n)
                    if nxt and n == 5:
                        copy_aT(nxt[0])
                    if later and n == 7:
                        copy_xT(later[0])
                    if prev:
                        if n == 0:
                            copy_yT(prev[0])
                        if n == 4:
                            copy_h2T(prev[0])
                    copy_pT(k, n)
                    if nxt:
                        if n == 0:
                            squares(nxt[0])
                        if n == 2:
                            q_relu(nxt[0])
                        if n == 5:
                            square_o(nxt[0])
                        if n == 7:
                            copy_hT(nxt[0])
                            keys(*nxt)
                    if later and n == 6:
                        copy_cT(later[0])
                    if prev and n == 5:
                        exp_gap(prev[0])

                def finish(k, u):
                    copy_yT(k)
                    copy_h2T(k)
                    exp_gap(k)

                act.wait_ge(consts, 1)
                act.wait_ge(w_ready, 1)
                schedule(act, opening, front, slot, finish)

                with act.Fori(0, E // 2) as rep:
                    for e in range(2):
                        act.wait_ge(b1_loaded[e], (rep + 1) * 16 * CH)
                        with act.Fori(0, GROUPS // 2) as r:
                            for u in LANES:
                                item = (rep * 2 + e) * GROUPS + r * 2 + u
                                for c in range(CH):
                                    act.wait_ge(mid_ps, item * CH + (c + 1))
                                    A(mid[u][:, c, :], bank[4 * u + c % 2][:, :], ACT.Gelu,
                                      bias=b1[e][:, c:c + 1]).then_inc(mid_ok, 1)

            @block.gpsimd
            def _(pool):
                G = nc.gpsimd
                steps = [0]

                def step(ins):
                    steps[0] += 1
                    ins.then_inc(setup, 1)
                    pool.wait_ge(setup, steps[0])

                def keep(ap, fill, compare, base, pattern, channel):
                    step(G.affine_select(out=ap, in_=ap, compare_op=compare, fill=fill, base=base,
                                         pattern=pattern, channel_multiplier=channel))

                step(G.memset(minus_half[:, :], -0.5))
                step(G.memset(ones_row[:, :], 1.0))
                step(G.iota(iota8[:, :], pattern=[[1, E]], base=0, channel_multiplier=0,
                            allow_small_or_imprecise_dtypes=True))
                for c in (ident, ident_bf):
                    step(G.memset(c[:, :], 0.0))
                    keep(c[:, :], 1.0, ALU.not_equal, 0, [[-1, P]], 1)
                step(G.memset(causal[:, :], 0.0))
                step(G.memset(batch2[:, :], 0.0))
                step(G.memset(head16[:, :], 1.0))
                step(G.memset(head8[:, :], 1.0))
                keep(head16[:, :], 0.0, ALU.is_ge, 0, [[-HD, HEADS]], 1)
                keep(head16[:, :], 0.0, ALU.is_ge, HD - 1, [[HD, HEADS]], -1)
                for b in range(BPT):
                    keep(causal[half(b), :], MASKED, ALU.is_ge, 0, [[-1, S]], 1)
                    keep(head8[half(b), :], 0.0, ALU.is_ge, 0, [[-HD, HG]], 1)
                    keep(head8[half(b), :], 0.0, ALU.is_ge, HD - 1, [[HD, HG]], -1)
                    step(G.memset(batch2[half(b), b:b + 1], 1.0))
                step(G.memset(kvz[:, :, :, :, :], 0.0))
                G.memset(xpb[:, 0, 0:1], 0.0).then_inc(consts, 1)

                def inv_sqrt(dst, src, n):
                    return G.tensor_tensor(dst, src, minus_half[:, 0:n], ALU.pow)

                def x_scale(k):
                    pool.wait_ge(x_var, k + 1)
                    inv_sqrt(x_rs[:, :], x_ve[:, :], T).then_inc(x_rstd, 1)

                def x_and_mask(k, u):
                    pool.wait_ge(m_loaded[u], (k // 2 + 1) * 16)
                    G.tensor_tensor(em2[:, :], em[u][:, :], em[u][:, :], ALU.mult).then_inc(em2_ok, 1)
                    pool.wait_ge(x_loaded[u], (k // 2 + 1) * 16)
                    if not (isinstance(k, int) and k == 0):
                        pool.wait_ge(x1_ok, k)
                    G.tensor_tensor(xpb[:, :, :], x_sb[u][:, :, :], over_t(beta_b[:, :]), ALU.add).then_inc(xpb_ok, 1)

                def qkv_scale(k):
                    pool.wait_ge(ss_ok, k + 1)
                    inv_sqrt(rs[:, :], ve[:, :], 3 * T).then_inc(qkv_rstd, 1)

                def values(k):
                    pool.wait_ge(vn_ok, k + 1)
                    pool.wait_ge(em2_ok, k + 1)
                    G.tensor_tensor(vp[:, :, :], vp[:, :, :], over_t(gamma_b[:, :]), ALU.mult).then_inc(vg_ok, 1)
                    pool.wait_ge(vg_ok, k + 1)
                    G.tensor_tensor(vp[:, :, :], vp[:, :, :], over_t(beta_b[:, :]), ALU.add).then_inc(vb_ok, 1)
                    pool.wait_ge(vb_ok, k + 1)
                    G.tensor_tensor(vp[:, :, :], vp[:, :, :], over_d(em2[:, :]), ALU.mult).then_inc(vp_ok, 1)

                def o_scale(k):
                    pool.wait_ge(oss_ok, k + 1)
                    inv_sqrt(rs[:, 0:T], ve[:, 0:T], T).then_inc(o_rstd, 1)

                def zh_scale(k):
                    pool.wait_ge(z_var, k + 1)
                    inv_sqrt(rs[:, 0:2 * T], ve[:, 0:2 * T], 2 * T).then_inc(z_rstd, 1)

                def z_bias(k, u):
                    pool.wait_ge(z_ok, k + 1)
                    G.tensor_tensor(zed[u][:, :, :], zed[u][:, :, :], over_t(bp_b[:, :]), ALU.add).then_inc(zb_ok, 1)

                def head_keys(k, u, n):
                    if n == 1:
                        pool.wait_ge(kf_ok, k + 1)
                    if not (isinstance(k, int) and k * UNITS + n < 2):
                        pool.wait_ge(s_ps, k * UNITS + (n - 1))
                    t = n // 2
                    G.tensor_tensor(km[n % 2][:, :, :],
                                    kb[u][:, n % 2, t * S:t * S + S].unsqueeze(1).broadcast_to([P, HG, S]),
                                    head8[:, :].unsqueeze(2).broadcast_to([P, HG, S]), ALU.mult).then_inc(km_ok, 1)

                def a_scale(k):
                    pool.wait_ge(a_var, k + 1)
                    inv_sqrt(e_rs[:, :], e_ve[:, :], T).then_inc(a_rstd, 1)

                def keep_residual(k, u):
                    pool.wait_ge(xa_ok, k + 1)
                    G.tensor_tensor(acc[:, k, :, :], x1[u][:, :, :], xa[:, :, :], ALU.add).then_inc(res_ok, 1)

                def opening(k, u):
                    x_scale(k)

                def front(k, u):
                    x_and_mask(k, u)
                    qkv_scale(k)
                    values(k)
                    o_scale(k)
                    zh_scale(k)
                    z_bias(k, u)
                    head_keys(k, u, 1)

                def slot(n, unit, nxt, later, prev):
                    k, u = unit
                    if prev and n == 2:
                        a_scale(prev[0])
                    if n + 2 < UNITS:
                        head_keys(k, u, n + 2)
                    if prev and n == 3:
                        keep_residual(*prev)
                    if nxt:
                        if n == 0:
                            x_and_mask(*nxt)
                        if n == 1:
                            qkv_scale(nxt[0])
                        if n == 2:
                            values(nxt[0])
                        if n == 5:
                            o_scale(nxt[0])
                    if later and n == 6:
                        x_scale(later[0])
                    if nxt:
                        if n == 6:
                            zh_scale(nxt[0])
                        if n == 7:
                            z_bias(*nxt)
                            head_keys(*nxt, 1)

                def finish(k, u):
                    a_scale(k)
                    keep_residual(k, u)

                schedule(pool, opening, front, slot, finish)

            @block.vector
            def _(dve):
                V = nc.vector
                F0, F1, F2 = front_bank

                def moments(src, st, out):
                    for t in range(T):
                        V.bn_stats(st[:, t, :], src[:, t, :])
                    dve.drain()
                    for t in range(T):
                        last = V.bn_aggr(out[:, t, :], st[:, t, :])
                    return last

                def normalize(dst, src, m, r):
                    for t in range(T):
                        last = V.tensor_scalar(dst[:, t, :], src[:, t, :], m[:, t, 0:1], r[:, t:t + 1],
                                               ALU.subtract, ALU.mult)
                    return last

                def x_moments(k, u):
                    dve.wait_ge(x_loaded[u], (k // 2 + 1) * 16)
                    moments(x_sb[u], stats, mv).then_inc(xs_b, 1)
                    dve.wait_ge(xs_b, k + 1)
                    V.tensor_scalar(x_ve[:, :], mv[:, :, 1], EPS_X, None, ALU.add).then_inc(x_var, 1)

                def x_normal(k, u):
                    dve.wait_ge(x_rstd, k + 1)
                    if not (isinstance(k, int) and k == 0):
                        dve.wait_ge(xT_ps, k)
                    normalize(xn, x_sb[u], mv, x_rs).then_inc(xn_ok, 1)

                def mask_columns(k, u):
                    dve.wait_ge(m_loaded[u], (k // 2 + 1) * 16)
                    V.tensor_tensor(emb[:, :, :], em[u][:, :].unsqueeze(2).broadcast_to([P, T, BPT]),
                                    batch2[:, :].unsqueeze(1).broadcast_to([P, T, BPT]), ALU.mult).then_inc(emb_ok, 1)

                def qkv_sums(k):
                    dve.wait_ge(sq_ok, k + 1)
                    V.tensor_reduce(ss[:, :], sq[:, :, :].rearrange("p w (t d) -> p (w t) d", t=T), AX.X,
                                    ALU.add).then_inc(sum_ok, 1)
                    dve.wait_ge(sum_ok, k + 1)
                    V.tensor_scalar(ve[:, :], ss[:, :], 1.0 / D, EPS_A, ALU.mult, ALU.add).then_inc(ss_ok, 1)

                def qkv_normal(k):
                    dve.wait_ge(qkv_rstd, k + 1)
                    for w, src, dst, ok in ((0, F2, qn, qn_ok), (2, F0, vp, vn_ok), (1, F1, kp, kn_ok)):
                        V.tensor_tensor(dst[:, :, :], t4(src[:, :]), over_d(rs[:, w * T:w * T + T]), ALU.mult)\
                            .then_inc(ok, 1)

                def keys_affine(k):
                    dve.wait_ge(kn_ok, k + 1)
                    V.tensor_tensor(kp[:, :, :], kp[:, :, :], over_t(gamma_b[:, :]), ALU.mult).then_inc(kg_ok, 1)
                    dve.wait_ge(kg_ok, k + 1)
                    V.tensor_tensor(kp[:, :, :], kp[:, :, :], over_t(beta_b[:, :]), ALU.add).then_inc(kb_ok, 1)
                    dve.wait_ge(kb_ok, k + 1)
                    V.tensor_scalar(kp[:, :, :], kp[:, :, :], 0.0, EPS_K, ALU.max, ALU.add).then_inc(kp_ok, 1)

                def q_eps(k):
                    dve.wait_ge(qr_ok, k + 1)
                    V.tensor_scalar(qp[:, :], qp[:, :], EPS_K, None, ALU.add).then_inc(qp_ok, 1)

                def key_values(k):
                    dve.wait_ge(ks_ps, k + 1)
                    V.tensor_tensor(
                        kvz[:, :, :, HD, 0:HEADS].rearrange("p t b h -> p (t b) h"),
                        F0[:, 0:T * BPT].unsqueeze(2).broadcast_to([P, T * BPT, HEADS]),
                        head16[:, :].unsqueeze(1).broadcast_to([P, T * BPT, HEADS]), ALU.mult)
                    dve.wait_ge(kv_ps, k + 1)
                    for b in range(BPT):
                        last = V.tensor_tensor(
                            kvz[:, :, b, 0:HD, 0:HEADS].rearrange("p t d h -> p t h d"),
                            front_bank[1 + b][:, :].rearrange("p (t h d) -> p t h d", t=T, h=HEADS),
                            head16[:, :].unsqueeze(1).unsqueeze(3).broadcast_to([P, T, HEADS, HD]), ALU.mult)
                    last.then_inc(kvz_ok, 1)

                def divide(k):
                    dve.wait_ge(au_ps, 2 * k + 2)
                    V.tensor_scalar(den[:, :, :], F2[:, 0:2 * S].rearrange("p (f n) -> p f n", f=2),
                                    EPS_K, None, ALU.add).then_inc(den_a, 1)
                    dve.wait_ge(den_a, k + 1)
                    V.reciprocal(den[:, :, :], den[:, :, :]).then_inc(den_b, 1)
                    dve.wait_ge(den_b, k + 1)
                    for part in range(2):
                        last = V.tensor_tensor(
                            att[:, part, :].rearrange("p (n e) -> p n e", e=HD),
                            front_bank[part][:, :].rearrange("p (e n) -> p n e", e=HD),
                            den[:, part, :].unsqueeze(2).broadcast_to([P, S, HD]), ALU.mult)
                    last.then_inc(att_ok, 1)

                def o_sums(k):
                    dve.wait_ge(o2_ok, k + 1)
                    V.tensor_reduce(ss[:, 0:T], t4(sq[:, 0, :]), AX.X, ALU.add).then_inc(osum_ok, 1)
                    dve.wait_ge(osum_ok, k + 1)
                    V.tensor_scalar(ve[:, 0:T], ss[:, 0:T], 1.0 / D, EPS_A, ALU.mult, ALU.add).then_inc(oss_ok, 1)

                def residual(k, u):
                    dve.wait_ge(o_rstd, k + 1)
                    for t in range(T):
                        last = V.scalar_tensor_tensor(out=x1[u][:, t, :], in0=t4(F1[:, :])[:, t, :],
                                                      scalar=rs[:, t:t + 1], in1=gamma_b[:, :],
                                                      op0=ALU.mult, op1=ALU.mult)
                    last.then_inc(og_ok, 1)
                    dve.wait_ge(og_ok, k + 1)
                    dve.wait_ge(xpb_ok, k + 1)
                    V.tensor_tensor(x1[u][:, :, :], x1[u][:, :, :], xpb[:, :, :], ALU.add).then_inc(x1_ok, 1)
                    dve.wait_ge(x1_ok, k + 1)
                    moments(x1[u], x1_stats, x1_mv).then_inc(zs_b, 1)
                    dve.wait_ge(zs_b, k + 1)
                    V.tensor_scalar(ve[:, 0:T], x1_mv[:, :, 1], EPS_X, None, ALU.add).then_inc(zv_a, 1)
                    dve.wait_ge(zv_a, k + 1)
                    V.reciprocal(rinv[:, :], ve[:, 0:T]).then_inc(zv_b, 1)
                    dve.wait_ge(zv_b, k + 1)
                    V.tensor_tensor(ve[:, T:2 * T], x1_mv[:, :, 1], rinv[:, :], ALU.mult).then_inc(zv_c, 1)
                    dve.wait_ge(zv_c, k + 1)
                    V.tensor_scalar(ve[:, T:2 * T], ve[:, T:2 * T], EPS_X, None, ALU.add).then_inc(z_var, 1)

                def z_normal(k, u):
                    dve.wait_ge(z_rstd, k + 1)
                    V.tensor_tensor(rprod[:, :], rs[:, 0:T], rs[:, T:2 * T], ALU.mult).then_inc(rp_ok, 1)
                    dve.wait_ge(rp_ok, k + 1)
                    normalize(hn, x1[u], x1_mv, rprod).then_inc(h_ok, 1)
                    normalize(zed[u], x1[u], x1_mv, rs).then_inc(z_ok, 1)

                def self_operands(k, u):
                    dve.wait_ge(qf_ps, k + 1)
                    for g in range(2):
                        for b in range(BPT):
                            last = V.tensor_scalar(
                                qbd[u][half(b), g, :, b * S:b * S + S],
                                F2[half(g), :].rearrange("p (t b s) -> p t b s", t=T, b=BPT)[:, :, b, :],
                                cols[half(g), BQ], SCALE, ALU.add, ALU.mult)
                    last.then_inc(qbd_ok, 1)
                    dve.wait_ge(kf_ok, k + 1)
                    if not (isinstance(k, int) and k == 0):
                        dve.wait_ge(s_ps, k * UNITS - 1)
                    V.tensor_tensor(km[0][:, :, :], kb[u][:, 0, 0:S].unsqueeze(1).broadcast_to([P, HG, S]),
                                    head8[:, :].unsqueeze(2).broadcast_to([P, HG, S]), ALU.mult).then_inc(km0_ok, 1)
                    dve.wait_ge(vf_ps, k + 1)
                    for odd in range(2):
                        for b in range(BPT):
                            last = V.tensor_tensor(
                                vbd[u][half(odd), :, b, :, odd * (HD + 1):odd * (HD + 1) + HD],
                                F0[half(b), :].rearrange("p (t h o d) -> p t h o d", t=T, o=2, d=HD)[:, :, :, odd, :],
                                bv_b[half(b), :].rearrange("p (h o d) -> p h o d", o=2, d=HD)[:, :, odd, :]
                                .unsqueeze(1).broadcast_to([S, T, HG, HD]), ALU.add)
                    last.then_inc(vbd_ok, 1)

                def score_max(k, n):
                    dve.wait_ge(s_ps, k * UNITS + (n + 1))
                    if not (isinstance(k, int) and k * UNITS + n < 2):
                        dve.wait_ge(sm_ps, k * UNITS + (n - 1))
                    V.tensor_reduce(mx[:, n % 2, :], score_bank[n % 2][:, :].rearrange("p (h k) -> p h k", h=HG),
                                    AX.X, ALU.max).then_inc(mx_ok, 1)

                def attended(k, u, n):
                    t = n // 2
                    pv = pv_bank[:, 0:HG * 4 * (HD + 1)].rearrange("p (h b o c) -> p h b o c", h=HG, b=BPT, o=2)
                    dve.wait_ge(pv_ps, k * UNITS + (n + 1))
                    V.reciprocal(rden[:, :].rearrange("p (h o) -> p h o", o=2), pv[:, :, 0, :, HD]).then_inc(rden_ok, 1)
                    dve.wait_ge(rden_ok, k * T + (t + 1))
                    for b in range(BPT):
                        last = V.tensor_tensor(
                            y[u][half(b), t, :].rearrange("p (h o d) -> p h o d", h=HG, o=2), pv[half(b), :, b, :, 0:HD],
                            rden[half(b), :].rearrange("p (h o) -> p h o", o=2).unsqueeze(3)
                            .broadcast_to([S, HG, 2, HD]), ALU.mult)
                    last.then_inc(y_ok, 1)

                def project_out(k, u):
                    dve.wait_ge(f_ps, k + 1)
                    dve.wait_ge(zb_ok, k + 1)
                    if not (isinstance(k, int) and k == 0):
                        dve.wait_ge(res_ok, k)
                    V.tensor_tensor(xa[:, :, :], t4(end_bank[:, :]), zed[u][:, :, :], ALU.add).then_inc(xa_ok, 1)
                    dve.wait_ge(xa_ok, k + 1)
                    moments(xa, e_stats, e_mv).then_inc(as_b, 1)
                    dve.wait_ge(as_b, k + 1)
                    V.tensor_scalar(e_ve[:, :], e_mv[:, :, 1], EPS_X, None, ALU.add).then_inc(a_var, 1)

                def a_normal(k):
                    dve.wait_ge(a_rstd, k + 1)
                    normalize(an, xa, e_mv, e_rs).then_inc(a_ok, 1)

                def keep_h2T(k):
                    dve.wait_ge(h2T_ok, k + 1)
                    V.tensor_copy(h2T[:, k, :], hgT[:, :, :].rearrange("p t n -> p (t n)")).then_inc(kept_ok, 1)

                def top_two(k):
                    dve.wait_ge(lg_ps, k + 1)
                    V.tensor_copy(logits[:, :, :], end_bank[:, 0:T * E].rearrange("p (t e) -> p t e", t=T))\
                        .then_inc(lg_ok, 1)
                    dve.drain()
                    for t in range(T):
                        last = V.max(top[:, t, :], logits[:, t, :])
                    last.then_inc(top_ok, 1)
                    dve.wait_ge(top_ok, k + 1)
                    V.tensor_tensor(dlt[:, :], top[:, :, 1], top[:, :, 0], ALU.subtract).then_inc(dl_ok, 1)
                    for t in range(T):
                        last = V.max_index(topi[:, t, :], top[:, t, :], logits[:, t, :])
                    last.then_inc(topi_ok, 1)

                def gates(k):
                    dve.wait_ge(topi_ok, k + 1)
                    V.tensor_copy(topf[:, :, :], topi[:, :, 0:2]).then_inc(hot_a, 1)
                    dve.wait_ge(e_ok, k + 1)
                    V.tensor_scalar(wgt[:, 2, :], dlt[:, :], 1.0, None, ALU.add).then_inc(wsum_ok, 1)
                    dve.wait_ge(hot_a, k + 1)
                    for j in range(2):
                        last = V.tensor_tensor(hot[:, j, :, :], iota8[:, :].unsqueeze(1).broadcast_to([P, T, E]),
                                               topf[:, :, j:j + 1].broadcast_to([P, T, E]), ALU.is_equal)
                    last.then_inc(hot_b, 1)
                    dve.wait_ge(wsum_ok, k + 1)
                    V.reciprocal(wgt[:, 0, :], wgt[:, 2, :]).then_inc(winv_ok, 1)
                    dve.wait_ge(winv_ok, k + 1)
                    V.tensor_tensor(wgt[:, 1, :], wgt[:, 0, :], dlt[:, :], ALU.mult).then_inc(wpair_ok, 1)
                    dve.wait_ge(wpair_ok, k + 1)
                    V.tensor_tensor(hot[:, :, :, :].rearrange("p k t e -> p (k t) e"),
                                    hot[:, :, :, :].rearrange("p k t e -> p (k t) e"),
                                    wgt[:, 0:2, :].rearrange("p k t -> p (k t)").unsqueeze(2)
                                    .broadcast_to([P, 2 * T, E]), ALU.mult).then_inc(hotw_ok, 1)
                    dve.wait_ge(hotw_ok, k + 1)
                    V.tensor_tensor(gate[:, k, :, :], hot[:, 0, :, :], hot[:, 1, :, :], ALU.add).then_inc(gate_ok, 1)

                def opening(k, u):
                    x_moments(k, u)
                    x_normal(k, u)

                def front(k, u):
                    mask_columns(k, u)
                    qkv_sums(k)
                    qkv_normal(k)
                    keys_affine(k)
                    q_eps(k)
                    key_values(k)
                    divide(k)
                    o_sums(k)
                    residual(k, u)
                    z_normal(k, u)
                    self_operands(k, u)

                def slot(n, unit, nxt, later, prev):
                    k, u = unit
                    if n == 0:
                        score_max(k, 0)
                    if n + 1 < UNITS:
                        score_max(k, n + 1)
                    if prev and n == 3:
                        a_normal(prev[0])
                    if nxt:
                        if n == 0:
                            mask_columns(*nxt)
                        if n == 1:
                            qkv_sums(nxt[0])
                        if n == 2:
                            qkv_normal(nxt[0])
                            keys_affine(nxt[0])
                        if n == 3:
                            q_eps(nxt[0])
                        if n == 4:
                            divide(nxt[0])
                    if prev:
                        if n == 1:
                            project_out(*prev)
                        if n == 5:
                            keep_h2T(prev[0])
                            top_two(prev[0])
                        if n == 6:
                            gates(prev[0])
                    if later and n == 6:
                        x_moments(*later)
                    if nxt and n == 6:
                        residual(*nxt)
                    if later and n == 7:
                        x_normal(*later)
                    if nxt and n == 7:
                        z_normal(*nxt)
                    if n % 2:
                        attended(k, u, n)
                    if nxt:
                        if n == 3:
                            key_values(nxt[0])
                        if n == 5:
                            o_sums(nxt[0])
                        if n == 7:
                            self_operands(*nxt)

                def finish(k, u):
                    project_out(k, u)
                    a_normal(k)
                    keep_h2T(k)
                    top_two(k)
                    gates(k)

                V.memset(ones_r[:, :].bitcast(F32), 1.0)
                for u in LANES:
                    V.memset(qbd[u][:, :, :, :], 0.0)
                    V.memset(vbd[u][:, :, :, :, :], 0.0).then_inc(zeroed, 1)
                dve.wait_ge(zeroed, 2)
                for u in LANES:
                    for odd in range(2):
                        at = odd * (HD + 1) + HD
                        V.memset(vbd[u][half(odd), :, :, :, at:at + 1], 1.0)
                dve.wait_ge(w_loaded, 16 * len(weights))
                dve.wait_ge(consts, 1)
                V.tensor_reduce(w_sum[:, :], w_raw[:, :, :], AX.X, ALU.add)
                V.tensor_reduce(db_sum[:, :], db_raw[:, :], AX.X, ALU.add)
                V.tensor_scalar(neg_ident[:, :], ident[:, :], -1.0, None, ALU.mult).then_inc(centred, 1)
                dve.wait_ge(centred, 1)
                V.tensor_scalar(w_sum[:, :], w_sum[:, :], -1.0 / D, None, ALU.mult)
                V.tensor_scalar(db_sum[:, :], db_sum[:, :], -1.0 / D, None, ALU.mult).then_inc(centred, 1)
                dve.wait_ge(centred, 2)
                V.tensor_tensor(wx[:, :, :], w_raw[:, :, :], w_sum[:, :].unsqueeze(2).broadcast_to([P, 4, D]), ALU.add)
                V.tensor_scalar(db_row[:, :], db_raw[:, :], db_sum[:, :], None, ALU.add).then_inc(centred, 1)
                dve.wait_ge(centred, 3)
                V.tensor_copy(db_hi[:, :], db_row[:, :]).then_inc(centred, 1)
                dve.wait_ge(centred, 4)
                V.tensor_tensor(db_lo[:, :], db_row[:, :], db_hi[:, :].bitcast(F32), ALU.subtract).then_inc(w_ready, 1)

                schedule(dve, opening, front, slot, finish)

                V.memset(rden[:, 0:1], 0.0).then_inc(acc_ok, 2)
                dve.wait_ge(res_ok, GROUPS)
                with dve.Fori(0, E // 2) as rep:
                    for e in range(2):
                        with dve.Fori(0, GROUPS // 2) as r:
                            for u in LANES:
                                item = (rep * 2 + e) * GROUPS + r * 2 + u
                                dve.wait_ge(y2_ps, item + 1)
                                for t in range(T):
                                    last = V.scalar_tensor_tensor(
                                        out=acc[:, r * 2 + u, t, :], in0=t4(bank[4 * u + 2][:, :])[:, t, :],
                                        scalar=gate[:, r * 2 + u, t, bass.ts(rep * 2 + e, 1)],
                                        in1=acc[:, r * 2 + u, t, :], op0=ALU.mult, op1=ALU.add)
                                last.then_inc(acc_ok, 1)


_INS = ['x', 'ctx_1024', 'mask_BxS2_ff1', 'L0_xattn_wq', 'L0_xattn_wk', 'L0_xattn_wv', 'L0_xattn_ln_gamma',
        'L0_xattn_ln_beta', 'L0_xattn_dense_w', 'L0_xattn_dense_b', 'L0_ffn_ln1_g', 'L0_ffn_ln1_b', 'L0_ffn_ln2_g',
        'L0_ffn_ln2_b', 'L0_ffn_Wq', 'L0_ffn_bq', 'L0_ffn_Wk', 'L0_ffn_bk', 'L0_ffn_Wv', 'L0_ffn_bv', 'L0_ffn_Wp',
        'L0_ffn_bp', 'L0_ffn_gate_W', 'L0_ffn_gate_b', 'L0_ffn_exp_W1', 'L0_ffn_exp_b1', 'L0_ffn_exp_W2',
        'L0_ffn_exp_b2']


def kernel(**inputs):
    import numpy as _np
    import concourse.bacc as _bacc
    from concourse import mybir as _mybir
    from concourse.bass_utils import run_bass_kernel_spmd as _run

    nc = _bacc.Bacc("TRN2", target_bir_lowering=False, num_devices=1)
    arrays, args = {}, {}
    for name in _INS:
        arr = _np.ascontiguousarray(inputs[name])
        arrays[f"in_{name}_dram"] = arr
        args[name] = nc.dram_tensor(f"in_{name}_dram", arr.shape, _mybir.dt.from_np(arr.dtype), kind="ExternalInput").ap()
    out = nc.dram_tensor("out_0_dram", (64, 64, 128), _mybir.dt.float32, kind="ExternalOutput").ap()
    xattn_attention_moe(nc, args, out)
    r = _run(nc, [arrays], core_ids=[0])
    return r.results[0]["out_0_dram"]
```

```python
from contextlib import ExitStack

import concourse.bass as bass
from concourse import mybir

ALU = mybir.AluOpType
ACT = mybir.ActivationFunctionType
AX = mybir.AxisListType
F32 = mybir.dt.float32
F32R = mybir.dt.float32r
BF16 = mybir.dt.bfloat16
U32 = mybir.dt.uint32

P = 128
LANES = (0, 1)
EPS_X = 1e-5
EPS_K = 1e-6
EPS_A = 1e-6
MASKED = -1e30


def xattn_attention_moe(nc: bass.Bass, a, out):
    B, S, D = a["x"].shape
    HEADS = 16
    HD = D // HEADS
    TILES = B * S // P
    T = 4
    N = T * P
    GROUPS = TILES // T
    E, _, H = a["L0_ffn_exp_W1"].shape
    CH = H // P
    BPT = P // S
    HG = HEADS // 2
    UNITS = 2 * T
    SCALE = float(HD) ** -0.5
    assert D == P and BPT == 2 and HG * S == 512

    x_v = a["x"].rearrange("(g t b) s d -> g (b s) t d", t=T, b=BPT)
    ctx_v = a["ctx_1024"].rearrange("(g t b) s d -> g (b s) t d", t=T, b=BPT)
    w2_v = a["L0_ffn_exp_W2"].rearrange("e (c p) d -> e p c d", p=P)
    b1_v = a["L0_ffn_exp_b1"].rearrange("e (c p o) -> e c p o", p=P, o=1)
    em_v = a["mask_BxS2_ff1"].rearrange("(g t b) s -> g (b s) t", t=T, b=BPT)
    out_v = out.rearrange("(g t b) s d -> g (b s) t d", t=T, b=BPT)

    with ExitStack() as ctx:
        def sb(name, shape, dt=F32):
            return ctx.enter_context(nc.sbuf_tensor(name, shape, dt))

        def lanes(name, shape, dt=F32):
            return [sb(f"{name}{u}", shape, dt) for u in LANES]

        def sems(names):
            return [ctx.enter_context(nc.semaphore(n)) for n in names.split()]

        bank = [ctx.enter_context(nc.psum_tensor(f"bank{k}", [P, 512], F32)) for k in range(8)]
        score_bank, probT_bank, pv_bank, front_bank, end_bank = bank[0:2], bank[2], bank[3], bank[4:7], bank[7]

        ident = sb("ident", [P, P])
        ident_bf = sb("ident_bf", [P, P], BF16)
        neg_ident = sb("neg_ident", [P, P], F32R)
        causal = sb("causal", [P, S], BF16)
        head16 = sb("head16", [P, HEADS])
        head8 = sb("head8", [P, HG])
        batch2 = sb("batch2", [P, BPT])
        minus_half = sb("minus_half", [P, 3 * T])
        ones_row = sb("ones_row", [1, P])
        ones_col = sb("ones_col", [P, 1])
        ones_r = sb("ones_r", [1, P], F32R)
        iota8 = sb("iota8", [P, E])
        w_raw = sb("w_raw", [P, 4, D])
        w_sum = sb("w_sum", [P, 4])
        wx = sb("wx", [P, 4, D])
        den = sb("den", [P, 2, S])
        db_raw = den[0:1, :, :].rearrange("p f n -> p (f n)")
        db_sum = sb("db_sum", [1, 1])
        db_row = sb("db_row", [1, D])
        db_hi = sb("db_hi", [1, D], F32R)
        db_lo = sb("db_lo", [1, D], F32R)
        wf = sb("wf", [P, 4, D])
        gate_w = sb("gate_w", [P, E])
        gamma_b = sb("gamma_b", [P, D])
        beta_b = sb("beta_b", [P, D])
        bv_b = sb("bv_b", [P, D])
        bp_b = sb("bp_b", [P, D])
        cols = sb("cols", [P, 8])
        gb_row = sb("gb_row", [1, E])

        places = sb("places", [P, 6, 4, T, D])
        place = [places[:, i, :, :, :] for i in range(6)]
        accT = places[:, 0:2, :, :, :].rearrange("p i g t d -> p (i g) (t d)")
        x_sb, c_sb = [place[0][:, u, :, :] for u in LANES], [place[0][:, 2 + u, :, :] for u in LANES]
        xn, hn, qn, kp = (place[1][:, i, :, :] for i in range(4))
        xpb = place[2][:, 0, :, :]
        xnT, cT, qp = (place[2][:, i, :, :].rearrange("p t d -> p (t d)") for i in (1, 2, 3))
        zed, y = [place[3][:, u, :, :] for u in LANES], [place[3][:, 2 + u, :, :] for u in LANES]

        sq = place[4][:, 0:3, :, :].rearrange("p w t d -> p w (t d)")
        vp = place[4][:, 3, :, :]
        att = place[5][:, 0:2, :, :].rearrange("p w t d -> p w (t d)")
        xa, an = place[5][:, 2, :, :], place[5][:, 3, :, :]

        em = lanes("em", [P, T])
        em2 = sb("em2", [P, T])
        emb = sb("emb", [P, T, BPT])
        stats = sb("stats", [P, T, 6])
        mv = sb("mv", [P, T, 2])
        x_ve = sb("x_ve", [P, T])
        x_rs = sb("x_rs", [P, T])
        x1_stats = sb("x1_stats", [P, T, 6])
        x1_mv = sb("x1_mv", [P, T, 2])
        ve = sb("ve", [P, 3 * T])
        rs = sb("rs", [P, 3 * T])
        ss = sb("ss", [P, 3 * T])
        kvz = sb("kvz", [P, T, BPT, HD + 1, 32])
        x1 = lanes("x1", [P, T, D])
        h1T = sb("h1T", [P, T, P])
        kb = lanes("kb", [P, 2, T * S])

        qbd = lanes("qbd", [P, 2, T, P])
        km = lanes("km", [P, HG, S])
        vbd = lanes("vbd", [P, T, BPT, HG, 2 * (HD + 1)])
        mx = sb("mx", [P, 2, HG], F32R)
        pr = sb("pr", [P, 2, 512])
        pT = sb("pT", [P, 4, P])
        rden = sb("rden", [P, HEADS])

        yT = w_raw[:, :, :].rearrange("p w d -> p (w d)")
        e_stats = sb("e_stats", [P, T, 6])
        e_mv = sb("e_mv", [P, T, 2])
        e_ve = sb("e_ve", [P, T])
        e_rs = sb("e_rs", [P, T])
        hgT = sb("hgT", [P, T, P])
        logits = sb("logits", [P, T, E])
        top = sb("top", [P, T, 8])
        topi = sb("topi", [P, T, 8], U32)
        topf = sb("topf", [P, T, 2])
        dlt = sb("dlt", [P, T])
        wgt = sb("wgt", [P, 3, T])
        hot = sb("hot", [P, 2, T, E])

        h2T_hi = sb("h2T_hi", [P, GROUPS, N], F32R)
        h2T_lo = sb("h2T_lo", [P, GROUPS, N], F32R)
        acc = sb("acc", [P, GROUPS, T, D])
        gate = sb("gate", [P, T, GROUPS, E])

        w1 = [place[2][:, e, :, :].rearrange("p t d -> p (t d)") for e in range(2)]
        w2 = [place[2][:, 2 + e, :, :] for e in range(2)]
        b1 = [sb(f"b1_{e}", [P, CH]) for e in range(2)]
        b2 = [sb(f"b2_{e}", [P, 1]) for e in range(2)]
        w1_hi, w1_lo = ([sb(f"w1_{e}_{part}", [P, H], F32R) for e in range(2)] for part in ("hi", "lo"))
        w2_hi, w2_lo = ([sb(f"w2_{e}_{part}", [P, CH, D], F32R) for e in range(2)] for part in ("hi", "lo"))
        gate_row = pT[0:GROUPS * E, :, :].rearrange("p j q -> p (j q)")
        gate_all = [x1[u][:, :, :].rearrange("p t d -> p (t d)") for u in LANES]
        gated = [pr[:, u, :] for u in LANES]
        mid = [place[4 + u][:, :, :, :].rearrange("p c t d -> p c (t d)") for u in LANES]
        mid_hi = lanes("mid_hi", [P, CH, N], F32R)
        mid_lo = lanes("mid_lo", [P, CH, N], F32R)

        (w_loaded, cT_ps, em2_ok, emb_ok, xpb_ok, xn_ok, kf_ok, gate_row_ok, gates_stored, gated_ok, out_ok,
         stored, xT_ok, lg_ok, cT_ok, xT_ps, k_ps, qbd_ok, q_ps, vbd_ok, v_ps, qn_ok, qT_ps, kp_ok, vn_ok,
         ks_ps, vp_ok, qr_ok, kv_ps, kvz_ok, qp_ok, au_ps, att_ok, aT_ps, aT_ok, o_ps, h_ok, hT_ps, hT_ok,
         kf_ps, qf_ps, vf_ps, km0_ok, km_ok, s_ps, mx_ok, sm_ps, p_ok, pT_ps, pT_ok, y_ok, pv_ps, yT_ps, yT_ok,
         f_ps, a_ok, aT2_ps, h2T_ok, lg_ps, consts, w_ready, gate_ok, res_ok, gate_row_ps, mid_ps, mid_lo_ok,
         y2_ps, acc_ok, fin_ps, sq_ok, o2_ok, h2T_hi_ok, dl_ok, e_ok, mid_ok, setup, x_var, x_rstd, x1_ok,
         ss_ok, qkv_rstd, vg_ok, vb_ok, oss_ok, o_rstd, z_var, z_rstd, z_ok, zb_ok, a_var, a_rstd, xa_ok, xs_b,
         sum_ok, kn_ok, kg_ok, kb_ok, den_a, den_b, osum_ok, og_ok, zs_b, kb0_ok, rden_ok, as_b, kept_ok,
         top_ok, topi_ok, hot_a, wsum_ok, hot_b, winv_ok, wpair_ok, hotw_ok, zeroed, centred) = sems(
            "w_loaded cT_ps em2_ok emb_ok xpb_ok xn_ok kf_ok gate_row_ok gates_stored gated_ok out_ok stored "
            "xT_ok lg_ok cT_ok xT_ps k_ps qbd_ok q_ps vbd_ok v_ps qn_ok qT_ps kp_ok vn_ok ks_ps vp_ok qr_ok "
            "kv_ps kvz_ok qp_ok au_ps att_ok aT_ps aT_ok o_ps h_ok hT_ps hT_ok kf_ps qf_ps vf_ps km0_ok km_ok "
            "s_ps mx_ok sm_ps p_ok pT_ps pT_ok y_ok pv_ps yT_ps yT_ok f_ps a_ok aT2_ps h2T_ok lg_ps consts "
            "w_ready gate_ok res_ok gate_row_ps mid_ps mid_lo_ok y2_ps acc_ok fin_ps sq_ok o2_ok h2T_hi_ok "
            "dl_ok e_ok mid_ok setup x_var x_rstd x1_ok ss_ok qkv_rstd vg_ok vb_ok oss_ok o_rstd z_var z_rstd "
            "z_ok zb_ok a_var a_rstd xa_ok xs_b sum_ok kn_ok kg_ok kb_ok den_a den_b osum_ok og_ok zs_b kb0_ok "
            "rden_ok as_b kept_ok top_ok topi_ok hot_a wsum_ok hot_b winv_ok wpair_ok hotw_ok zeroed centred")
        c_loaded = sems("c_loaded0 c_loaded1")
        x_loaded = sems("x_loaded0 x_loaded1")
        m_loaded = sems("m_loaded0 m_loaded1")
        w1_loaded = sems("w1_loaded0 w1_loaded1")
        w2_loaded = sems("w2_loaded0 w2_loaded1")
        b2_loaded = sems("b2_loaded0 b2_loaded1")
        b1_loaded = sems("b1_loaded0 b1_loaded1")
        gate_loaded = sems("gate_loaded0 gate_loaded1")
        w_split = sems("w_split0 w_split1")
        w1_hi_ok = sems("w1_hi_ok0 w1_hi_ok1")
        w2_hi_ok = sems("w2_hi_ok0 w2_hi_ok1")
        w1_lo_ok = sems("w1_lo_ok0 w1_lo_ok1")

        def col(v):
            return v.rearrange("(p o) -> p o", o=1)

        def row(v):
            return v.rearrange("(o n) -> o n", o=1)

        def t4(ap):
            return ap.rearrange("p (t d) -> p t d", t=T)

        def over_d(ap):
            return ap.unsqueeze(2).broadcast_to([P, ap.shape[1], D])

        def over_t(ap):
            return ap.unsqueeze(1).broadcast_to([ap.shape[0], T, ap.shape[1]])

        def half(b):
            return slice(b * S, b * S + S)

        G1, B1, G2, B2, BQ, BK, GX, BX = (slice(i, i + 1) for i in range(8))
        weights = [
            (w_raw[:, 0, :], a["L0_xattn_wq"]), (w_raw[:, 1, :], a["L0_xattn_wk"]),
            (w_raw[:, 2, :], a["L0_xattn_wv"]), (w_raw[:, 3, :], a["L0_xattn_dense_w"]),
            (db_raw[:, :], row(a["L0_xattn_dense_b"])),
            (gamma_b[:, :], row(a["L0_xattn_ln_gamma"]).broadcast_to([P, D])),
            (beta_b[:, :], row(a["L0_xattn_ln_beta"]).broadcast_to([P, D])),
            (cols[:, GX], col(a["L0_xattn_ln_gamma"])), (cols[:, BX], col(a["L0_xattn_ln_beta"])),
            (wf[:, 0, :], a["L0_ffn_Wq"]), (wf[:, 1, :], a["L0_ffn_Wk"]), (wf[:, 2, :], a["L0_ffn_Wv"]),
            (wf[:, 3, :], a["L0_ffn_Wp"]), (gate_w[:, :], a["L0_ffn_gate_W"]),
            (bv_b[:, :], row(a["L0_ffn_bv"]).broadcast_to([P, D])),
            (bp_b[:, :], row(a["L0_ffn_bp"]).broadcast_to([P, D])),
            (cols[:, G1], col(a["L0_ffn_ln1_g"])), (cols[:, B1], col(a["L0_ffn_ln1_b"])),
            (cols[:, G2], col(a["L0_ffn_ln2_g"])), (cols[:, B2], col(a["L0_ffn_ln2_b"])),
            (cols[:, BQ], col(a["L0_ffn_bq"])), (cols[:, BK], col(a["L0_ffn_bk"])),
            (gb_row[:, :], row(a["L0_ffn_gate_b"])),
        ]

        def schedule(eng, opening, front, slot, finish):
            def beat(k, u, first=False):
                nxt = None if isinstance(k, int) and k + 1 >= GROUPS else (k + 1, 1 - u)
                later = None if isinstance(k, int) and k + 2 >= GROUPS else (k + 2, u)
                prev = None if first else (k - 1, 1 - u)
                for n in range(UNITS):
                    slot(n, (k, u), nxt, later, prev)

            opening(0, 0)
            front(0, 0)
            opening(1, 1)
            beat(0, 0, first=True)
            with eng.Fori(0, GROUPS // 2 - 2) as r:
                beat(2 * r + 1, 1)
                beat(2 * r + 2, 0)
            for k in range(GROUPS - 3, GROUPS):
                beat(k, k % 2)
            finish(GROUPS - 1, 1)

        gate_dram = nc.dram_tensor("gate_rows", (GROUPS * E, N), F32, kind="Internal").ap()
        gate_v = gate_dram.rearrange("(g e) (o n) -> e g o n", e=E, o=1)

        with nc.Block() as block:
            @block.sync
            def _(sp):
                for dst, src in weights:
                    sp.dma_start(dst, src).then_inc(w_loaded, 16)

                def load(u, group):
                    sp.dma_start(c_sb[u][:, :, :], ctx_v[group]).then_inc(c_loaded[u], 16)
                    sp.dma_start(x_sb[u][:, :, :], x_v[group]).then_inc(x_loaded[u], 16)
                    sp.dma_start(em[u][:, :], em_v[group], allow_slow_non_contiguous=True).then_inc(m_loaded[u], 16)

                for u in LANES:
                    load(u, u)

                def load_expert(e, expert):
                    sp.dma_start(w1[e][:, :], a["L0_ffn_exp_W1"][expert]).then_inc(w1_loaded[e], 16)
                    sp.dma_start(w2[e][:, :, :], w2_v[expert]).then_inc(w2_loaded[e], 16)
                    sp.dma_start(b2[e][:, :], a["L0_ffn_exp_b2"].rearrange("e (d o) -> e d o", o=1)[expert])\
                      .then_inc(b2_loaded[e], 16)
                    for c in range(CH):
                        sp.dma_start(b1[e][:, c:c + 1], b1_v[expert][c]).then_inc(b1_loaded[e], 16)

                with sp.Fori(0, GROUPS // 2 - 1) as r:
                    for u in LANES:
                        k = 2 * r + u
                        sp.wait_ge(cT_ps, k + 1)
                        sp.wait_ge(em2_ok, k + 1)
                        sp.wait_ge(emb_ok, k + 1)
                        sp.wait_ge(xpb_ok, k + 1)
                        sp.wait_ge(xn_ok, k + 1)
                        load(u, k + 2)

                sp.wait_ge(kf_ok, GROUPS)
                for e in range(2):
                    load_expert(e, e)

                sp.wait_ge(gate_row_ok, 1)
                sp.dma_start(gate_dram, gate_row[:, :]).then_inc(gates_stored, 16)
                sp.wait_ge(gates_stored, 16)

                def load_gates(rep, e):
                    with sp.Fori(0, GROUPS // 2) as r:
                        for u in LANES:
                            sp.wait_ge(gated_ok, (rep * 2 + e) * GROUPS + r * 2 + u + 1)
                            sp.dma_start(gate_all[u][:, :], gate_v[rep * 2 + e][r * 2 + u].broadcast_to([P, N]))\
                              .then_inc(gate_loaded[u], 16)

                with sp.Fori(0, E // 2 - 1) as rep:
                    for e in range(2):
                        load_gates(rep, e)
                        sp.wait_ge(gated_ok, (rep * 2 + e + 1) * GROUPS + 2)
                        load_expert(e, rep * 2 + e + 2)
                for e in range(2):
                    load_gates(E // 2 - 1, e)
                for g in range(GROUPS):
                    sp.wait_ge(out_ok, g + 1)
                    sp.dma_start(out_v[g], acc[:, g, :, :]).then_inc(stored, 16)
                sp.wait_ge(stored, 16 * GROUPS)

            @block.tensor
            def _(pe):
                F0, F1, F2 = front_bank

                def per_tile(psum, lhsT, rhs):
                    for t in range(T):
                        last = pe.matmul(t4(psum[:, :])[:, t, :], lhsT[:, t * P:t * P + P], rhs, start=True, stop=True)
                    return last

                def transposes(psum, src):
                    for t in range(T):
                        last = pe.transpose(t4(psum[:, :])[:, t, :], src[:, t, :], ident[:, :])
                    return last

                def context_T(k, u):
                    pe.wait_ge(c_loaded[u], (k // 2 + 1) * 16)
                    if isinstance(k, int) and k == 1:
                        pe.wait_ge(xT_ok, 1)
                    elif not (isinstance(k, int) and k < 3):
                        pe.wait_ge(lg_ok, k - 2)
                    transposes(end_bank, c_sb[u]).then_inc(cT_ps, 1)

                def x_T(k):
                    pe.wait_ge(xn_ok, k + 1)
                    pe.wait_ge(cT_ok, k + 1)
                    transposes(end_bank, xn).then_inc(xT_ps, 1)

                def project_k(k):
                    pe.wait_ge(cT_ok, k + 1)
                    if not (isinstance(k, int) and k == 0):
                        pe.wait_ge(kf_ok, k)
                    per_tile(F1, cT, wx[:, 1, :]).then_inc(k_ps, 1)

                def project_q(k):
                    pe.wait_ge(xT_ok, k + 1)
                    if not (isinstance(k, int) and k == 0):
                        pe.wait_ge(qbd_ok, 2 * k)
                    per_tile(F2, xnT, wx[:, 0, :]).then_inc(q_ps, 1)

                def project_v(k):
                    if not (isinstance(k, int) and k == 0):
                        pe.wait_ge(vbd_ok, k)
                    per_tile(F0, cT, wx[:, 2, :]).then_inc(v_ps, 1)

                def q_T(k):
                    pe.wait_ge(qn_ok, k + 1)
                    transposes(F2, qn).then_inc(qT_ps, 1)

                def key_sums(k):
                    pe.wait_ge(kp_ok, k + 1)
                    pe.wait_ge(emb_ok, k + 1)
                    pe.wait_ge(vn_ok, k + 1)
                    for t in range(T):
                        last = pe.matmul(F0[:, t * BPT:t * BPT + BPT], kp[:, t, :], emb[:, t, :], start=True, stop=True)
                    last.then_inc(ks_ps, 1)

                def key_values(k):
                    pe.wait_ge(vp_ok, k + 1)
                    pe.wait_ge(qr_ok, k + 1)
                    for b in range(BPT):
                        for t in range(T):
                            last = pe.matmul(t4(front_bank[1 + b][:, :])[:, t, :], kp[half(b), t, :],
                                             vp[half(b), t, :], start=True, stop=True)
                    last.then_inc(kv_ps, 1)

                def linear_attention(k, part):
                    if part == 0:
                        pe.wait_ge(kvz_ok, k + 1)
                        pe.wait_ge(qp_ok, k + 1)
                    for c in range(HD + 1):
                        dst, at = (front_bank[part], c * S) if c < HD else (F2, part * S)
                        for b4 in range(4):
                            t, b = 2 * part + b4 // 2, b4 % 2
                            last = pe.matmul(dst[b4 * 32:b4 * 32 + 32, at:at + S], kvz[:, t, b, c, :],
                                             qp[:, t * P + b * S:t * P + b * S + S], start=True, stop=True)
                    last.then_inc(au_ps, 1)

                def attention_T(k):
                    pe.wait_ge(att_ok, k + 1)
                    for part in range(2):
                        for n4 in range(4):
                            last = pe.transpose((F2, F0)[part][:, n4 * P:n4 * P + P],
                                                att[:, part, n4 * P:n4 * P + P], ident[:, :])
                    last.then_inc(aT_ps, 1)

                def dense(k):
                    pe.wait_ge(aT_ok, k + 1)
                    pe.matmul(t4(F1[:, :]), ones_r[:, :], over_t(db_hi[:, :]), start=True, stop=True)
                    pe.matmul(t4(F1[:, :]), ones_r[:, :], over_t(db_lo[:, :]), start=False, stop=True,
                              skip_group_check=True)
                    for t in range(T):
                        last = pe.matmul(t4(F1[:, :])[:, t, :], xnT[:, t * P:t * P + P], wx[:, 3, :],
                                         start=False, stop=True, skip_group_check=True)
                    last.then_inc(o_ps, 1)

                def h_T(k):
                    pe.wait_ge(h_ok, k + 1)
                    transposes(F0, hn).then_inc(hT_ps, 1)

                def project_self(k):
                    pe.wait_ge(hT_ok, k + 1)
                    h = h1T[:, :, :].rearrange("p t n -> p (t n)")
                    pe.matmul(F1[:, :], wf[:, 1, :], h, start=True, stop=True).then_inc(kf_ps, 1)
                    pe.matmul(F2[:, :], wf[:, 0, :], h, start=True, stop=True).then_inc(qf_ps, 1)
                    per_tile(F0, h, wf[:, 2, :]).then_inc(vf_ps, 1)

                def scores(k, u, n):
                    if n == 0:
                        pe.wait_ge(qbd_ok, 2 * k + 1)
                        pe.wait_ge(km0_ok, k + 1)
                    else:
                        if n == 1:
                            pe.wait_ge(qbd_ok, 2 * k + 2)
                        pe.wait_ge(km_ok, k * (UNITS - 1) + n)
                    bank_n = score_bank[n % 2]
                    pe.matmul(bank_n[:, :], ident_bf[:, :], causal[:, :].unsqueeze(1).broadcast_to([P, HG, S]),
                              start=True, stop=False)
                    pe.matmul(bank_n[:, :], qbd[u][:, n % 2, n // 2, :], km[n % 2][:, :, :],
                              start=False, stop=True).then_inc(s_ps, 1)

                def subtract_max(k, n):
                    pe.wait_ge(mx_ok, k * UNITS + (n + 1))
                    pe.matmul(score_bank[n % 2][:, :], neg_ident[:, :],
                              mx[:, n % 2, :].unsqueeze(2).broadcast_to([P, HG, S]),
                              start=False, stop=True, skip_group_check=True).then_inc(sm_ps, 1)

                def probs_T(k, n):
                    pe.wait_ge(p_ok, k * UNITS + (n + 1))
                    for j in range(4):
                        last = pe.transpose(probT_bank[:, j * P:j * P + P], pr[:, n % 2, j * P:j * P + P], ident[:, :])
                    last.then_inc(pT_ps, 1)

                def probs_values(k, u, n):
                    t = n // 2
                    pe.wait_ge(pT_ok, k * UNITS + (n + 1))
                    if n == 0:
                        pe.wait_ge(vbd_ok, k + 1)
                    if n % 2 == 0 and not (isinstance(k, int) and k * T + t == 0):
                        pe.wait_ge(y_ok, k * T + t)
                    W = 2 * BPT * (HD + 1)
                    for j in range(4):
                        hp = (n % 2) * 4 + j
                        last = pe.matmul(pv_bank[:, hp * W:hp * W + W].rearrange("p (b c) -> p b c", b=BPT),
                                         pT[:, j, :], vbd[u][:, t, :, hp, :], start=True, stop=True)
                    last.then_inc(pv_ps, 1)

                def y_T(k, u):
                    pe.wait_ge(y_ok, (k + 1) * T)
                    opened = k + 3
                    pe.wait_ge(xT_ok, min(opened, GROUPS) if isinstance(k, int) else opened)
                    if not (isinstance(k, int) and k == 0):
                        pe.wait_ge(lg_ok, k)
                    transposes(end_bank, y[u]).then_inc(yT_ps, 1)

                def project_out(k):
                    pe.wait_ge(yT_ok, k + 1)
                    per_tile(end_bank, yT, wf[:, 3, :]).then_inc(f_ps, 1)

                def a_T(k):
                    pe.wait_ge(a_ok, k + 1)
                    transposes(end_bank, an).then_inc(aT2_ps, 1)

                def gate_logits(k):
                    pe.wait_ge(h2T_ok, k + 1)
                    lg = end_bank[:, 0:T * E].rearrange("p (t e) -> p t e", t=T)
                    pe.matmul(lg, ones_row[:, :], over_t(gb_row[:, :]), start=True, stop=True)
                    for t in range(T):
                        last = pe.matmul(lg[:, t, :], hgT[:, t, :], gate_w[:, :], start=False, stop=True,
                                         skip_group_check=True)
                    last.then_inc(lg_ps, 1)

                def opening(k, u):
                    context_T(k, u)
                    x_T(k)

                def front(k, u):
                    project_k(k)
                    project_q(k)
                    project_v(k)
                    q_T(k)
                    key_sums(k)
                    key_values(k)
                    linear_attention(k, 0)
                    linear_attention(k, 1)
                    attention_T(k)
                    dense(k)
                    h_T(k)
                    project_self(k)

                def slot(n, unit, nxt, later, prev):
                    k, u = unit
                    if n == 0:
                        scores(k, u, 0)
                    subtract_max(k, n)
                    if n + 1 < UNITS:
                        if not (isinstance(k, int) and k * UNITS + n == 0):
                            pe.wait_ge(p_ok, k * UNITS + n)
                        scores(k, u, n + 1)
                    if n >= 1:
                        probs_values(k, u, n - 1)
                    if prev:
                        if n == 0:
                            y_T(*prev)
                        if n == 1:
                            project_out(prev[0])
                        if n == 6:
                            gate_logits(prev[0])
                    if nxt:
                        if n == 0:
                            project_k(nxt[0])
                            project_q(nxt[0])
                        if n == 3:
                            q_T(nxt[0])
                        if n == 4:
                            linear_attention(nxt[0], 0)
                        if n == 5:
                            attention_T(nxt[0])
                    if later and n == 7:
                        context_T(*later)
                    probs_T(k, n)
                    if nxt:
                        if n == 0:
                            project_v(nxt[0])
                        if n == 3:
                            key_sums(nxt[0])
                            key_values(nxt[0])
                        if n == 4:
                            linear_attention(nxt[0], 1)
                        if n == 5:
                            dense(nxt[0])
                    if prev and n == 5:
                        a_T(prev[0])
                    if n == UNITS - 1:
                        probs_values(k, u, n)
                    if later and n == 7:
                        x_T(later[0])
                    if nxt and n == 7:
                        h_T(nxt[0])
                        project_self(nxt[0])

                def finish(k, u):
                    y_T(k, u)
                    project_out(k)
                    a_T(k)
                    gate_logits(k)

                pe.wait_ge(consts, 1)
                pe.wait_ge(w_ready, 1)
                schedule(pe, opening, front, slot, finish)

                pe.wait_ge(gate_ok, GROUPS)
                pe.wait_ge(res_ok, GROUPS)
                for t in range(T):
                    last = pe.transpose(bank[3][0:GROUPS * E, t * P:t * P + P],
                                        gate[:, t, :, :].rearrange("p g e -> p (g e)"), ident[:, :])
                last.then_inc(gate_row_ps, 1)

                def three_passes(dst, hi_lo_w, hi_lo_x, start, stop):
                    for n, (w, x) in enumerate(((0, 0), (1, 0), (0, 1))):
                        last = pe.matmul(dst, hi_lo_w[w], hi_lo_x[x], start=start and n == 0, stop=stop and n == 2)
                    return last

                def middle(rep, e, r, c):
                    if c == 0:
                        pe.wait_ge(w_split[e], rep + 1)
                    chunk = slice(c * P, c * P + P)
                    for u in LANES:
                        three_passes(bank[4 * u + c % 2][:, :], (w1_hi[e][:, chunk], w1_lo[e][:, chunk]),
                                     (h2T_hi[:, r * 2 + u, :], h2T_lo[:, r * 2 + u, :]), True, True).then_inc(mid_ps, 1)

                def output(rep, e, r, c):
                    for u in LANES:
                        item = (rep * 2 + e) * GROUPS + r * 2 + u
                        part = ((rep * 2 + e) * GROUPS + r * 2) * CH + c * 2 + u
                        if c == 0:
                            pe.wait_ge(gated_ok, item + 1)
                        pe.wait_ge(mid_lo_ok, part + 1)
                        last = three_passes(bank[4 * u + 2][:, :], (w2_hi[e][:, c, :], w2_lo[e][:, c, :]),
                                            (mid_hi[u][:, c, :], mid_lo[u][:, c, :]), c == 0, c == CH - 1)
                        if c == CH - 1:
                            last.then_inc(y2_ps, 1)

                def pair(rep, e, r, following):
                    for c in range(CH):
                        if c + 1 < CH:
                            middle(rep, e, r, c + 1)
                        elif following:
                            middle(*following, 0)
                        output(rep, e, r, c)

                def expert(rep, e, following):
                    with pe.Fori(0, GROUPS // 2 - 1) as r:
                        pair(rep, e, r, (rep, e, r + 1))
                    pair(rep, e, GROUPS // 2 - 1, following)

                middle(0, 0, 0, 0)
                with pe.Fori(0, E // 2 - 1) as rep:
                    expert(rep, 0, (rep, 1, 0))
                    expert(rep, 1, (rep + 1, 0, 0))
                expert(E // 2 - 1, 0, (E // 2 - 1, 1, 0))
                expert(E // 2 - 1, 1, None)

                for g in range(GROUPS):
                    pe.wait_ge(acc_ok, (E - 1) * GROUPS + g + 3)
                    if g >= 2:
                        pe.wait_ge(out_ok, g - 1)
                    for t in range(T):
                        last = pe.transpose(bank[3 + 4 * (g % 2)][:, t * P:t * P + P], accT[:, g, t * P:t * P + P],
                                            ident[:, :])
                    last.then_inc(fin_ps, 1)

            @block.scalar
            def _(act):
                A = nc.scalar.activation
                F0, F1, F2 = front_bank

                def copy_cT(k):
                    act.wait_ge(cT_ps, k + 1)
                    if not (isinstance(k, int) and k == 0):
                        act.wait_ge(v_ps, k)
                    nc.scalar.copy(cT[:, :], end_bank[:, :]).then_inc(cT_ok, 1)

                def copy_xT(k):
                    act.wait_ge(xT_ps, k + 1)
                    if not (isinstance(k, int) and k == 0):
                        act.wait_ge(o_ps, k)
                    nc.scalar.copy(xnT[:, :], end_bank[:, :]).then_inc(xT_ok, 1)

                def squares(k):
                    for w, src, ready in ((1, F1, k_ps), (0, F2, q_ps), (2, F0, v_ps)):
                        act.wait_ge(ready, k + 1)
                        last = A(sq[:, w, :], src[:, :], ACT.Square)
                    last.then_inc(sq_ok, 1)

                def q_relu(k):
                    act.wait_ge(qT_ps, k + 1)
                    A(qp[:, :], F2[:, :], ACT.Relu, bias=cols[:, BX], scale=cols[:, GX]).then_inc(qr_ok, 1)

                def copy_aT(k):
                    act.wait_ge(aT_ps, k + 1)
                    for part in range(2):
                        last = nc.scalar.copy(
                            xnT[:, part * 256:part * 256 + 256].rearrange("p (b h n) -> p n b h", b=4, n=4),
                            (F2, F0)[part][:, :].rearrange("p (n b x h) -> p n b x h", n=4, b=4, x=2)[:, :, :, 0, :])
                    last.then_inc(aT_ok, 1)

                def square_o(k):
                    act.wait_ge(o_ps, k + 1)
                    A(sq[:, 0, :], F1[:, :], ACT.Square).then_inc(o2_ok, 1)

                def copy_hT(k):
                    act.wait_ge(hT_ps, k + 1)
                    A(h1T[:, :, :], t4(F0[:, :]), ACT.Identity, bias=cols[:, B1], scale=cols[:, G1]).then_inc(hT_ok, 1)

                def keys(k, u):
                    act.wait_ge(kf_ps, k + 1)
                    for g in range(2):
                        for b in range(BPT):
                            last = A(kb[u][half(b), g, :].rearrange("p (t s) -> p t s", t=T),
                                     F1[half(g), :].rearrange("p (t b s) -> p t b s", t=T, b=BPT)[:, :, b, :],
                                     ACT.Identity, bias=cols[half(g), BK])
                        last.then_inc((kb0_ok, kf_ok)[g], 1)

                def exp_scores(k, n):
                    act.wait_ge(sm_ps, k * UNITS + (n + 1))
                    A(pr[:, n % 2, :], score_bank[n % 2][:, :], ACT.Exp).then_inc(p_ok, 1)

                def copy_pT(k, n):
                    act.wait_ge(pT_ps, k * UNITS + (n + 1))
                    if not (isinstance(k, int) and k * UNITS + n == 0):
                        act.wait_ge(pv_ps, k * UNITS + n)
                    nc.scalar.copy(pT[:, :, :], probT_bank[:, :].rearrange("p (j q) -> p j q", j=4)).then_inc(pT_ok, 1)

                def copy_yT(k):
                    act.wait_ge(yT_ps, k + 1)
                    nc.scalar.copy(yT[:, :], end_bank[:, :]).then_inc(yT_ok, 1)

                def copy_h2T(k):
                    act.wait_ge(aT2_ps, k + 1)
                    A(hgT[:, :, :], t4(end_bank[:, :]), ACT.Identity, bias=cols[:, B2], scale=cols[:, G2])\
                        .then_inc(h2T_ok, 1)

                def round_h2T(k):
                    act.wait_ge(h2T_ok, k + 1)
                    nc.scalar.copy(h2T_hi[:, k, :], hgT[:, :, :].rearrange("p t n -> p (t n)")).then_inc(h2T_hi_ok, 1)

                def exp_gap(k):
                    act.wait_ge(dl_ok, k + 1)
                    A(dlt[:, :], dlt[:, :], ACT.Exp).then_inc(e_ok, 1)

                def opening(k, u):
                    copy_cT(k)
                    copy_xT(k)

                def front(k, u):
                    squares(k)
                    q_relu(k)
                    copy_aT(k)
                    square_o(k)
                    copy_hT(k)
                    keys(k, u)

                def slot(n, unit, nxt, later, prev):
                    k, u = unit
                    exp_scores(k, n)
                    if nxt and n == 3:
                        q_relu(nxt[0])
                    if nxt and n == 5:
                        copy_aT(nxt[0])
                    if later and n == 7:
                        copy_cT(later[0])
                    if prev and n == 0:
                        copy_yT(prev[0])
                    copy_pT(k, n)
                    if nxt:
                        if n == 0:
                            squares(nxt[0])
                        if n == 5:
                            square_o(nxt[0])
                    if prev:
                        if n == 5:
                            copy_h2T(prev[0])
                        if n == 6:
                            round_h2T(prev[0])
                        if n == 7:
                            exp_gap(prev[0])
                    if later and n == 7:
                        copy_xT(later[0])
                    if nxt and n == 7:
                        copy_hT(nxt[0])
                        keys(*nxt)

                def finish(k, u):
                    copy_yT(k)
                    copy_h2T(k)
                    round_h2T(k)
                    exp_gap(k)

                act.wait_ge(consts, 1)
                act.wait_ge(w_ready, 1)
                schedule(act, opening, front, slot, finish)

                act.wait_ge(gate_row_ps, 1)
                nc.scalar.copy(gate_row[:, :], bank[3][0:GROUPS * E, :]).then_inc(gate_row_ok, 1)

                with act.Fori(0, E // 2) as rep:
                    for e in range(2):
                        act.wait_ge(b1_loaded[e], (rep + 1) * 16 * CH)
                        with act.Fori(0, GROUPS // 2) as r:
                            for c in range(CH):
                                for u in LANES:
                                    part = ((rep * 2 + e) * GROUPS + r * 2) * CH + c * 2 + u
                                    act.wait_ge(mid_ps, part + 1)
                                    for dst in (mid, mid_hi):
                                        last = A(dst[u][:, c, :], bank[4 * u + c % 2][:, :], ACT.Gelu,
                                                 bias=b1[e][:, c:c + 1])
                                    last.then_inc(mid_ok, 1)

            @block.gpsimd
            def _(pool):
                G = nc.gpsimd
                steps = [0]

                def step(ins):
                    steps[0] += 1
                    ins.then_inc(setup, 1)
                    pool.wait_ge(setup, steps[0])

                def keep(ap, fill, compare, base, pattern, channel):
                    step(G.affine_select(out=ap, in_=ap, compare_op=compare, fill=fill, base=base,
                                         pattern=pattern, channel_multiplier=channel))

                step(G.memset(minus_half[:, :], -0.5))
                step(G.memset(ones_row[:, :], 1.0))
                step(G.memset(ones_col[:, :], 1.0))
                step(G.iota(iota8[:, :], pattern=[[1, E]], base=0, channel_multiplier=0,
                            allow_small_or_imprecise_dtypes=True))
                for c in (ident, ident_bf):
                    step(G.memset(c[:, :], 0.0))
                    keep(c[:, :], 1.0, ALU.not_equal, 0, [[-1, P]], 1)
                step(G.memset(causal[:, :], 0.0))
                step(G.memset(batch2[:, :], 0.0))
                step(G.memset(head16[:, :], 1.0))
                step(G.memset(head8[:, :], 1.0))
                keep(head16[:, :], 0.0, ALU.is_ge, 0, [[-HD, HEADS]], 1)
                keep(head16[:, :], 0.0, ALU.is_ge, HD - 1, [[HD, HEADS]], -1)
                for b in range(BPT):
                    keep(causal[half(b), :], MASKED, ALU.is_ge, 0, [[-1, S]], 1)
                    keep(head8[half(b), :], 0.0, ALU.is_ge, 0, [[-HD, HG]], 1)
                    keep(head8[half(b), :], 0.0, ALU.is_ge, HD - 1, [[HD, HG]], -1)
                    step(G.memset(batch2[half(b), b:b + 1], 1.0))
                step(G.memset(kvz[:, :, :, :, :], 0.0))
                G.memset(xpb[:, 0, 0:1], 0.0).then_inc(consts, 1)

                def inv_sqrt(dst, src, n):
                    return G.tensor_tensor(dst, src, minus_half[:, 0:n], ALU.pow)

                def x_scale(k):
                    pool.wait_ge(x_var, k + 1)
                    inv_sqrt(x_rs[:, :], x_ve[:, :], T).then_inc(x_rstd, 1)

                def x_and_mask(k, u):
                    pool.wait_ge(m_loaded[u], (k // 2 + 1) * 16)
                    G.tensor_tensor(em2[:, :], em[u][:, :], em[u][:, :], ALU.mult).then_inc(em2_ok, 1)
                    pool.wait_ge(x_loaded[u], (k // 2 + 1) * 16)
                    if not (isinstance(k, int) and k == 0):
                        pool.wait_ge(x1_ok, k)
                    G.tensor_tensor(xpb[:, :, :], x_sb[u][:, :, :], over_t(beta_b[:, :]), ALU.add).then_inc(xpb_ok, 1)

                def qkv_scale(k):
                    pool.wait_ge(ss_ok, k + 1)
                    inv_sqrt(rs[:, :], ve[:, :], 3 * T).then_inc(qkv_rstd, 1)

                def values(k):
                    pool.wait_ge(vn_ok, k + 1)
                    pool.wait_ge(em2_ok, k + 1)
                    G.tensor_tensor(vp[:, :, :], vp[:, :, :], over_t(gamma_b[:, :]), ALU.mult).then_inc(vg_ok, 1)
                    pool.wait_ge(vg_ok, k + 1)
                    G.tensor_tensor(vp[:, :, :], vp[:, :, :], over_t(beta_b[:, :]), ALU.add).then_inc(vb_ok, 1)
                    pool.wait_ge(vb_ok, k + 1)
                    G.tensor_tensor(vp[:, :, :], vp[:, :, :], over_d(em2[:, :]), ALU.mult).then_inc(vp_ok, 1)

                def o_scale(k):
                    pool.wait_ge(oss_ok, k + 1)
                    inv_sqrt(rs[:, 0:T], ve[:, 0:T], T).then_inc(o_rstd, 1)

                def zh_scale(k):
                    pool.wait_ge(z_var, k + 1)
                    inv_sqrt(rs[:, 0:2 * T], ve[:, 0:2 * T], 2 * T).then_inc(z_rstd, 1)

                def z_bias(k, u):
                    pool.wait_ge(z_ok, k + 1)
                    G.tensor_tensor(zed[u][:, :, :], zed[u][:, :, :], over_t(bp_b[:, :]), ALU.add).then_inc(zb_ok, 1)

                def head_keys(k, u, n):
                    if n == 1:
                        pool.wait_ge(kf_ok, k + 1)
                    if not (isinstance(k, int) and k * UNITS + n < 2):
                        pool.wait_ge(s_ps, k * UNITS + (n - 1))
                    t = n // 2
                    G.tensor_tensor(km[n % 2][:, :, :],
                                    kb[u][:, n % 2, t * S:t * S + S].unsqueeze(1).broadcast_to([P, HG, S]),
                                    head8[:, :].unsqueeze(2).broadcast_to([P, HG, S]), ALU.mult).then_inc(km_ok, 1)

                def a_scale(k):
                    pool.wait_ge(a_var, k + 1)
                    inv_sqrt(e_rs[:, :], e_ve[:, :], T).then_inc(a_rstd, 1)

                def keep_residual(k, u):
                    pool.wait_ge(xa_ok, k + 1)
                    G.tensor_tensor(acc[:, k, :, :], x1[u][:, :, :], xa[:, :, :], ALU.add).then_inc(res_ok, 1)

                def split_weights(e, times):
                    pool.wait_ge(w1_loaded[e], times * 16)
                    G.tensor_tensor(w1_hi[e][:, :], w1[e][:, :], ones_col[:, :].broadcast_to([P, H]), ALU.mult).then_inc(w1_hi_ok[e], 1)
                    pool.wait_ge(w2_loaded[e], times * 16)
                    G.tensor_tensor(w2_hi[e][:, :, :], w2[e][:, :, :], ones_col[:, :].unsqueeze(2)
                                    .broadcast_to([P, CH, D]), ALU.mult).then_inc(w2_hi_ok[e], 1)
                    pool.wait_ge(w1_hi_ok[e], times)
                    G.tensor_tensor(w1_lo[e][:, :], w1[e][:, :], w1_hi[e][:, :].bitcast(F32), ALU.subtract)\
                        .then_inc(w1_lo_ok[e], 1)
                    pool.wait_ge(w2_hi_ok[e], times)
                    pool.wait_ge(w1_lo_ok[e], times)
                    G.tensor_tensor(w2_lo[e][:, :, :], w2[e][:, :, :], w2_hi[e][:, :, :].bitcast(F32), ALU.subtract)\
                     .then_inc(w_split[e], 1)

                def opening(k, u):
                    x_scale(k)

                def front(k, u):
                    x_and_mask(k, u)
                    qkv_scale(k)
                    values(k)
                    o_scale(k)
                    zh_scale(k)
                    head_keys(k, u, 1)

                def slot(n, unit, nxt, later, prev):
                    k, u = unit
                    if not nxt and n == 5:
                        split_weights(0, 1)
                    if not nxt and n == 6:
                        G.memset(accT[:, :, :], 0.0).then_inc(acc_ok, 2)
                    for unit_n in {0: (2,), 1: (3,), 3: (6,), 4: (7,)}.get(n, ()):
                        head_keys(k, u, unit_n)
                    if prev and n == 3:
                        a_scale(prev[0])
                        keep_residual(*prev)
                    if n == 0:
                        z_bias(k, u)
                    if later and n == 5:
                        x_scale(later[0])
                    if nxt:
                        if n == 0:
                            x_and_mask(*nxt)
                        if n == 1:
                            qkv_scale(nxt[0])
                        if n == 2:
                            values(nxt[0])
                    if n == 1:
                        head_keys(k, u, 4)
                    if n == 2:
                        head_keys(k, u, 5)
                    if nxt:
                        if n == 5:
                            o_scale(nxt[0])
                        if n == 6:
                            zh_scale(nxt[0])
                        if n == 7:
                            head_keys(*nxt, 1)

                def finish(k, u):
                    a_scale(k)
                    keep_residual(k, u)

                schedule(pool, opening, front, slot, finish)

                def accumulate(rep, e, first, end):
                    with pool.Fori(first, end) as r:
                        for u in LANES:
                            item = (rep * 2 + e) * GROUPS + r * 2 + u
                            pool.wait_ge(gated_ok, item + 3)
                            G.tensor_tensor(accT[:, r * 2 + u, :], accT[:, r * 2 + u, :], gated[u][:, :], ALU.add)\
                                .then_inc(acc_ok, 1)

                def expert(rep, e, more):
                    accumulate(rep, e, 0, GROUPS // 4)
                    if more:
                        split_weights(1 - e, rep + 1 + e)
                    accumulate(rep, e, GROUPS // 4, GROUPS // 2)

                with pool.Fori(0, E // 2 - 1) as rep:
                    expert(rep, 0, True)
                    expert(rep, 1, True)
                expert(E // 2 - 1, 0, True)
                expert(E // 2 - 1, 1, False)

            @block.vector
            def _(dve):
                V = nc.vector
                F0, F1, F2 = front_bank

                def moments(src, st, out):
                    for t in range(T):
                        V.bn_stats(st[:, t, :], src[:, t, :])
                    dve.drain()
                    for t in range(T):
                        last = V.bn_aggr(out[:, t, :], st[:, t, :])
                    return last

                def normalize(dst, src, m, r):
                    for t in range(T):
                        last = V.tensor_scalar(dst[:, t, :], src[:, t, :], m[:, t, 0:1], r[:, t:t + 1],
                                               ALU.subtract, ALU.mult)
                    return last

                def x_moments(k, u):
                    dve.wait_ge(x_loaded[u], (k // 2 + 1) * 16)
                    moments(x_sb[u], stats, mv).then_inc(xs_b, 1)
                    dve.wait_ge(xs_b, k + 1)
                    V.tensor_scalar(x_ve[:, :], mv[:, :, 1], EPS_X, None, ALU.add).then_inc(x_var, 1)

                def x_normal(k, u):
                    dve.wait_ge(x_rstd, k + 1)
                    if not (isinstance(k, int) and k == 0):
                        dve.wait_ge(xT_ps, k)
                    normalize(xn, x_sb[u], mv, x_rs).then_inc(xn_ok, 1)

                def mask_columns(k, u):
                    dve.wait_ge(m_loaded[u], (k // 2 + 1) * 16)
                    V.tensor_tensor(emb[:, :, :], em[u][:, :].unsqueeze(2).broadcast_to([P, T, BPT]),
                                    batch2[:, :].unsqueeze(1).broadcast_to([P, T, BPT]), ALU.mult).then_inc(emb_ok, 1)

                def qkv_sums(k):
                    dve.wait_ge(sq_ok, k + 1)
                    V.tensor_reduce(ss[:, :], sq[:, :, :].rearrange("p w (t d) -> p (w t) d", t=T), AX.X,
                                    ALU.add).then_inc(sum_ok, 1)
                    dve.wait_ge(sum_ok, k + 1)
                    V.tensor_scalar(ve[:, :], ss[:, :], 1.0 / D, EPS_A, ALU.mult, ALU.add).then_inc(ss_ok, 1)

                def qkv_normal(k):
                    dve.wait_ge(qkv_rstd, k + 1)
                    for w, src, dst, ok in ((0, F2, qn, qn_ok), (2, F0, vp, vn_ok), (1, F1, kp, kn_ok)):
                        V.tensor_tensor(dst[:, :, :], t4(src[:, :]), over_d(rs[:, w * T:w * T + T]), ALU.mult)\
                            .then_inc(ok, 1)

                def keys_affine(k):
                    dve.wait_ge(kn_ok, k + 1)
                    V.tensor_tensor(kp[:, :, :], kp[:, :, :], over_t(gamma_b[:, :]), ALU.mult).then_inc(kg_ok, 1)
                    dve.wait_ge(kg_ok, k + 1)
                    V.tensor_tensor(kp[:, :, :], kp[:, :, :], over_t(beta_b[:, :]), ALU.add).then_inc(kb_ok, 1)
                    dve.wait_ge(kb_ok, k + 1)
                    V.tensor_scalar(kp[:, :, :], kp[:, :, :], 0.0, EPS_K, ALU.max, ALU.add).then_inc(kp_ok, 1)

                def q_eps(k):
                    dve.wait_ge(qr_ok, k + 1)
                    V.tensor_scalar(qp[:, :], qp[:, :], EPS_K, None, ALU.add).then_inc(qp_ok, 1)

                def key_values(k):
                    dve.wait_ge(ks_ps, k + 1)
                    V.tensor_tensor(
                        kvz[:, :, :, HD, 0:HEADS].rearrange("p t b h -> p (t b) h"),
                        F0[:, 0:T * BPT].unsqueeze(2).broadcast_to([P, T * BPT, HEADS]),
                        head16[:, :].unsqueeze(1).broadcast_to([P, T * BPT, HEADS]), ALU.mult)
                    dve.wait_ge(kv_ps, k + 1)
                    for b in range(BPT):
                        last = V.tensor_tensor(
                            kvz[:, :, b, 0:HD, 0:HEADS].rearrange("p t d h -> p t h d"),
                            front_bank[1 + b][:, :].rearrange("p (t h d) -> p t h d", t=T, h=HEADS),
                            head16[:, :].unsqueeze(1).unsqueeze(3).broadcast_to([P, T, HEADS, HD]), ALU.mult)
                    last.then_inc(kvz_ok, 1)

                def divide(k):
                    dve.wait_ge(au_ps, 2 * k + 2)
                    V.tensor_scalar(den[:, :, :], F2[:, 0:2 * S].rearrange("p (f n) -> p f n", f=2),
                                    EPS_K, None, ALU.add).then_inc(den_a, 1)
                    dve.wait_ge(den_a, k + 1)
                    V.reciprocal(den[:, :, :], den[:, :, :]).then_inc(den_b, 1)
                    dve.wait_ge(den_b, k + 1)
                    for part in range(2):
                        last = V.tensor_tensor(
                            att[:, part, :].rearrange("p (n e) -> p n e", e=HD),
                            front_bank[part][:, :].rearrange("p (e n) -> p n e", e=HD),
                            den[:, part, :].unsqueeze(2).broadcast_to([P, S, HD]), ALU.mult)
                    last.then_inc(att_ok, 1)

                def o_sums(k):
                    dve.wait_ge(o2_ok, k + 1)
                    V.tensor_reduce(ss[:, 0:T], t4(sq[:, 0, :]), AX.X, ALU.add).then_inc(osum_ok, 1)
                    dve.wait_ge(osum_ok, k + 1)
                    V.tensor_scalar(ve[:, 0:T], ss[:, 0:T], 1.0 / D, EPS_A, ALU.mult, ALU.add).then_inc(oss_ok, 1)

                def residual(k, u):
                    dve.wait_ge(o_rstd, k + 1)
                    for t in range(T):
                        last = V.scalar_tensor_tensor(out=x1[u][:, t, :], in0=t4(F1[:, :])[:, t, :],
                                                      scalar=rs[:, t:t + 1], in1=gamma_b[:, :],
                                                      op0=ALU.mult, op1=ALU.mult)
                    last.then_inc(og_ok, 1)
                    dve.wait_ge(og_ok, k + 1)
                    dve.wait_ge(xpb_ok, k + 1)
                    V.tensor_tensor(x1[u][:, :, :], x1[u][:, :, :], xpb[:, :, :], ALU.add).then_inc(x1_ok, 1)
                    dve.wait_ge(x1_ok, k + 1)
                    moments(x1[u], x1_stats, x1_mv).then_inc(zs_b, 1)
                    dve.wait_ge(zs_b, k + 1)
                    V.tensor_scalar(ve[:, 0:T], x1_mv[:, :, 1], EPS_X, None, ALU.add)
                    V.tensor_scalar(ve[:, T:2 * T], x1_mv[:, :, 1], 1.0 + EPS_X, EPS_X * EPS_X, ALU.mult, ALU.add)\
                     .then_inc(z_var, 1)

                def h_normal(k, u):
                    dve.wait_ge(z_rstd, k + 1)
                    normalize(hn, x1[u], x1_mv, rs[:, T:2 * T]).then_inc(h_ok, 1)

                def z_normal(k, u):
                    dve.wait_ge(z_rstd, k + 1)
                    normalize(zed[u], x1[u], x1_mv, rs).then_inc(z_ok, 1)

                def unit0_keys(k, u):
                    dve.wait_ge(kb0_ok, k + 1)
                    if not (isinstance(k, int) and k == 0):
                        dve.wait_ge(s_ps, k * UNITS - 1)
                    V.tensor_tensor(km[0][:, :, :], kb[u][:, 0, 0:S].unsqueeze(1).broadcast_to([P, HG, S]),
                                    head8[:, :].unsqueeze(2).broadcast_to([P, HG, S]), ALU.mult).then_inc(km0_ok, 1)

                def queries(k, u):
                    dve.wait_ge(qf_ps, k + 1)
                    for g in range(2):
                        for b in range(BPT):
                            last = V.tensor_scalar(
                                qbd[u][half(b), g, :, b * S:b * S + S],
                                F2[half(g), :].rearrange("p (t b s) -> p t b s", t=T, b=BPT)[:, :, b, :],
                                cols[half(g), BQ], SCALE, ALU.add, ALU.mult)
                        last.then_inc(qbd_ok, 1)

                def self_values(k, u):
                    dve.wait_ge(vf_ps, k + 1)
                    for odd in range(2):
                        for b in range(BPT):
                            last = V.tensor_tensor(
                                vbd[u][half(odd), :, b, :, odd * (HD + 1):odd * (HD + 1) + HD],
                                F0[half(b), :].rearrange("p (t h o d) -> p t h o d", t=T, o=2, d=HD)[:, :, :, odd, :],
                                bv_b[half(b), :].rearrange("p (h o d) -> p h o d", o=2, d=HD)[:, :, odd, :]
                                .unsqueeze(1).broadcast_to([S, T, HG, HD]), ALU.add)
                    last.then_inc(vbd_ok, 1)

                def score_max(k, n):
                    dve.wait_ge(s_ps, k * UNITS + (n + 1))
                    if not (isinstance(k, int) and k * UNITS + n < 2):
                        dve.wait_ge(sm_ps, k * UNITS + (n - 1))
                    V.tensor_reduce(mx[:, n % 2, :], score_bank[n % 2][:, :].rearrange("p (h k) -> p h k", h=HG),
                                    AX.X, ALU.max).then_inc(mx_ok, 1)

                def attended(k, u, n):
                    t = n // 2
                    pv = pv_bank[:, 0:HG * 4 * (HD + 1)].rearrange("p (h b o c) -> p h b o c", h=HG, b=BPT, o=2)
                    dve.wait_ge(pv_ps, k * UNITS + (n + 1))
                    V.reciprocal(rden[:, :].rearrange("p (h o) -> p h o", o=2), pv[:, :, 0, :, HD]).then_inc(rden_ok, 1)
                    dve.wait_ge(rden_ok, k * T + (t + 1))
                    for b in range(BPT):
                        last = V.tensor_tensor(
                            y[u][half(b), t, :].rearrange("p (h o d) -> p h o d", h=HG, o=2), pv[half(b), :, b, :, 0:HD],
                            rden[half(b), :].rearrange("p (h o) -> p h o", o=2).unsqueeze(3)
                            .broadcast_to([S, HG, 2, HD]), ALU.mult)
                    last.then_inc(y_ok, 1)

                def project_out(k, u):
                    dve.wait_ge(f_ps, k + 1)
                    dve.wait_ge(zb_ok, k + 1)
                    if not (isinstance(k, int) and k == 0):
                        dve.wait_ge(res_ok, k)
                    V.tensor_tensor(xa[:, :, :], t4(end_bank[:, :]), zed[u][:, :, :], ALU.add).then_inc(xa_ok, 1)
                    dve.wait_ge(xa_ok, k + 1)
                    moments(xa, e_stats, e_mv).then_inc(as_b, 1)
                    dve.wait_ge(as_b, k + 1)
                    V.tensor_scalar(e_ve[:, :], e_mv[:, :, 1], EPS_X, None, ALU.add).then_inc(a_var, 1)

                def a_normal(k):
                    dve.wait_ge(a_rstd, k + 1)
                    normalize(an, xa, e_mv, e_rs).then_inc(a_ok, 1)

                def keep_h2T(k):
                    dve.wait_ge(h2T_ok, k + 1)
                    dve.wait_ge(h2T_hi_ok, k + 1)
                    V.tensor_tensor(h2T_lo[:, k, :], hgT[:, :, :].rearrange("p t n -> p (t n)"),
                                    h2T_hi[:, k, :].bitcast(F32), ALU.subtract).then_inc(kept_ok, 1)

                def copy_logits(k):
                    dve.wait_ge(lg_ps, k + 1)
                    V.tensor_copy(logits[:, :, :], end_bank[:, 0:T * E].rearrange("p (t e) -> p t e", t=T))\
                        .then_inc(lg_ok, 1)

                def top_two(k):
                    dve.drain()
                    for t in range(T):
                        last = V.max(top[:, t, :], logits[:, t, :])
                    last.then_inc(top_ok, 1)
                    dve.wait_ge(top_ok, k + 1)
                    V.tensor_tensor(dlt[:, :], top[:, :, 1], top[:, :, 0], ALU.subtract).then_inc(dl_ok, 1)
                    for t in range(T):
                        last = V.max_index(topi[:, t, :], top[:, t, :], logits[:, t, :])
                    last.then_inc(topi_ok, 1)

                def gates(k):
                    dve.wait_ge(topi_ok, k + 1)
                    V.tensor_copy(topf[:, :, :], topi[:, :, 0:2]).then_inc(hot_a, 1)
                    dve.wait_ge(e_ok, k + 1)
                    V.tensor_scalar(wgt[:, 2, :], dlt[:, :], 1.0, None, ALU.add).then_inc(wsum_ok, 1)
                    dve.wait_ge(hot_a, k + 1)
                    for j in range(2):
                        last = V.tensor_tensor(hot[:, j, :, :], iota8[:, :].unsqueeze(1).broadcast_to([P, T, E]),
                                               topf[:, :, j:j + 1].broadcast_to([P, T, E]), ALU.is_equal)
                    last.then_inc(hot_b, 1)
                    dve.wait_ge(wsum_ok, k + 1)
                    V.reciprocal(wgt[:, 0, :], wgt[:, 2, :]).then_inc(winv_ok, 1)
                    dve.wait_ge(winv_ok, k + 1)
                    V.tensor_tensor(wgt[:, 1, :], wgt[:, 0, :], dlt[:, :], ALU.mult).then_inc(wpair_ok, 1)
                    dve.wait_ge(wpair_ok, k + 1)
                    V.tensor_tensor(hot[:, :, :, :].rearrange("p k t e -> p (k t) e"),
                                    hot[:, :, :, :].rearrange("p k t e -> p (k t) e"),
                                    wgt[:, 0:2, :].rearrange("p k t -> p (k t)").unsqueeze(2)
                                    .broadcast_to([P, 2 * T, E]), ALU.mult).then_inc(hotw_ok, 1)
                    dve.wait_ge(hotw_ok, k + 1)
                    V.tensor_tensor(gate[:, :, k, :], hot[:, 0, :, :], hot[:, 1, :, :], ALU.add).then_inc(gate_ok, 1)

                def opening(k, u):
                    x_moments(k, u)
                    x_normal(k, u)

                def front(k, u):
                    mask_columns(k, u)
                    qkv_sums(k)
                    qkv_normal(k)
                    keys_affine(k)
                    q_eps(k)
                    key_values(k)
                    divide(k)
                    o_sums(k)
                    residual(k, u)
                    h_normal(k, u)
                    unit0_keys(k, u)
                    queries(k, u)

                def slot(n, unit, nxt, later, prev):
                    k, u = unit
                    if n == 0:
                        score_max(k, 0)
                        self_values(k, u)
                    if n + 1 < UNITS:
                        score_max(k, n + 1)
                    if n % 2 == 0 and n:
                        attended(k, u, n - 1)
                    if n == 0:
                        z_normal(k, u)
                    if prev:
                        if n == 3:
                            project_out(*prev)
                        if n == 4:
                            a_normal(prev[0])
                        if n == 6:
                            copy_logits(prev[0])
                    if later:
                        if n == 5:
                            x_moments(*later)
                        if n == 7:
                            x_normal(*later)
                    if nxt:
                        if n == 0:
                            mask_columns(*nxt)
                        if n == 1:
                            qkv_sums(nxt[0])
                        if n == 2:
                            qkv_normal(nxt[0])
                            keys_affine(nxt[0])
                        if n == 3:
                            q_eps(nxt[0])
                        if n == 4:
                            divide(nxt[0])
                        if n == 6:
                            residual(*nxt)
                    if prev and n == 7:
                        keep_h2T(prev[0])
                        top_two(prev[0])
                    if nxt and n == 7:
                        h_normal(*nxt)
                    if n == UNITS - 1:
                        attended(k, u, n)
                    if prev and n == 7:
                        gates(prev[0])
                    if nxt:
                        if n == 3:
                            key_values(nxt[0])
                        if n == 5:
                            o_sums(nxt[0])
                        if n == 7:
                            unit0_keys(*nxt)
                            queries(*nxt)

                def finish(k, u):
                    project_out(k, u)
                    a_normal(k)
                    copy_logits(k)
                    keep_h2T(k)
                    top_two(k)
                    gates(k)

                V.memset(ones_r[:, :].bitcast(F32), 1.0)
                for u in LANES:
                    V.memset(qbd[u][:, :, :, :], 0.0)
                    V.memset(vbd[u][:, :, :, :, :], 0.0).then_inc(zeroed, 1)
                dve.wait_ge(zeroed, 2)
                for u in LANES:
                    for odd in range(2):
                        at = odd * (HD + 1) + HD
                        V.memset(vbd[u][half(odd), :, :, :, at:at + 1], 1.0)
                dve.wait_ge(w_loaded, 16 * len(weights))
                dve.wait_ge(consts, 1)
                V.tensor_reduce(w_sum[:, :], w_raw[:, :, :], AX.X, ALU.add)
                V.tensor_reduce(db_sum[:, :], db_raw[:, :], AX.X, ALU.add)
                V.tensor_scalar(neg_ident[:, :], ident[:, :], -1.0, None, ALU.mult).then_inc(centred, 1)
                dve.wait_ge(centred, 1)
                V.tensor_scalar(w_sum[:, :], w_sum[:, :], -1.0 / D, None, ALU.mult)
                V.tensor_scalar(db_sum[:, :], db_sum[:, :], -1.0 / D, None, ALU.mult).then_inc(centred, 1)
                dve.wait_ge(centred, 2)
                V.tensor_tensor(wx[:, :, :], w_raw[:, :, :], w_sum[:, :].unsqueeze(2).broadcast_to([P, 4, D]), ALU.add)
                V.tensor_scalar(db_row[:, :], db_raw[:, :], db_sum[:, :], None, ALU.add).then_inc(centred, 1)
                dve.wait_ge(centred, 3)
                V.tensor_copy(db_hi[:, :], db_row[:, :]).then_inc(centred, 1)
                dve.wait_ge(centred, 4)
                V.tensor_tensor(db_lo[:, :], db_row[:, :], db_hi[:, :].bitcast(F32), ALU.subtract).then_inc(w_ready, 1)

                schedule(dve, opening, front, slot, finish)

                V.memset(rden[:, 0:1], 0.0).then_inc(gated_ok, 2)
                with dve.Fori(0, E // 2) as rep:
                    for e in range(2):
                        with dve.Fori(0, GROUPS // 2) as r:
                            for c in range(CH):
                                for u in LANES:
                                    part = ((rep * 2 + e) * GROUPS + r * 2) * CH + c * 2 + u
                                    dve.wait_ge(mid_ok, part + 1)
                                    V.tensor_tensor(mid_lo[u][:, c, :], mid[u][:, c, :],
                                                    mid_hi[u][:, c, :].bitcast(F32), ALU.subtract)\
                                     .then_inc(mid_lo_ok, 1)
                            for u in LANES:
                                item = (rep * 2 + e) * GROUPS + r * 2 + u
                                dve.wait_ge(b2_loaded[e], (rep + 1) * 16)
                                dve.wait_ge(gate_loaded[u], ((rep * 2 + e) * (GROUPS // 2) + r + 1) * 16)
                                dve.wait_ge(acc_ok, item + 1)
                                dve.wait_ge(y2_ps, item + 1)
                                V.scalar_tensor_tensor(out=gated[u][:, :], in0=bank[4 * u + 2][:, :], scalar=b2[e][:, :],
                                                       in1=gate_all[u][:, :], op0=ALU.add, op1=ALU.mult)\
                                 .then_inc(gated_ok, 1)
                for g in range(GROUPS):
                    dve.wait_ge(fin_ps, g + 1)
                    V.tensor_tensor(acc[:, g, :, :], t4(bank[3 + 4 * (g % 2)][:, :]), acc[:, g, :, :], ALU.add)\
                        .then_inc(out_ok, 1)


_INS = ['x', 'ctx_1024', 'mask_BxS2_ff1', 'L0_xattn_wq', 'L0_xattn_wk', 'L0_xattn_wv', 'L0_xattn_ln_gamma',
        'L0_xattn_ln_beta', 'L0_xattn_dense_w', 'L0_xattn_dense_b', 'L0_ffn_ln1_g', 'L0_ffn_ln1_b', 'L0_ffn_ln2_g',
        'L0_ffn_ln2_b', 'L0_ffn_Wq', 'L0_ffn_bq', 'L0_ffn_Wk', 'L0_ffn_bk', 'L0_ffn_Wv', 'L0_ffn_bv', 'L0_ffn_Wp',
        'L0_ffn_bp', 'L0_ffn_gate_W', 'L0_ffn_gate_b', 'L0_ffn_exp_W1', 'L0_ffn_exp_b1', 'L0_ffn_exp_W2',
        'L0_ffn_exp_b2']


def kernel(**inputs):
    import numpy as _np
    import concourse.bacc as _bacc
    from concourse import mybir as _mybir
    from concourse.bass_utils import run_bass_kernel_spmd as _run

    nc = _bacc.Bacc("TRN2", target_bir_lowering=False, num_devices=1)
    arrays, args = {}, {}
    for name in _INS:
        arr = _np.ascontiguousarray(inputs[name])
        arrays[f"in_{name}_dram"] = arr
        args[name] = nc.dram_tensor(f"in_{name}_dram", arr.shape, _mybir.dt.from_np(arr.dtype), kind="ExternalInput").ap()
    out = nc.dram_tensor("out_0_dram", (64, 64, 128), _mybir.dt.float32, kind="ExternalOutput").ap()
    xattn_attention_moe(nc, args, out)
    r = _run(nc, [arrays], core_ids=[0])
    return r.results[0]["out_0_dram"]
```
